# Optimizing a Trainium2 kernel written in Bass

```python
import numpy as np
import jax
import jax.numpy as jnp

def _softmax(x, axis=-1):
    return jax.nn.softmax(x, axis=axis)

def _gelu(x):
    return jax.nn.gelu(x, approximate=True)

def _silu(x):
    return jax.nn.silu(x)

def _sigmoid(x):
    return jax.nn.sigmoid(x)

def _layernorm(x, axis=-1, eps=1e-05):
    m = jnp.mean(x, axis=axis, keepdims=True)
    v = jnp.var(x, axis=axis, keepdims=True)
    return (x - m) / jnp.sqrt(v + eps)

def _scatter_add(tgt, idx, src, axis=0):
    return tgt.at[idx].add(src)

def _segment_sum(src, seg, n):
    return jax.ops.segment_sum(src, seg, n)
kernel_name = 'mk_vit_tower_d1_tok_img1024_r4_00c221'

def setup_inputs(seed: int=0):
    np.random.seed(seed)
    _w = jnp.asarray

    def _rec_inputs():
        import jax
        import jax.numpy as jnp
        _rk = jax.random.key(seed)
        x = -0.000169711 + 1.00022 * jax.random.normal(jax.random.fold_in(_rk, 1), (64, 3, 84, 84), jnp.float32)
        return x
    x = _rec_inputs()

    def _L0_tok_setup():
        import jax, jax.numpy as jnp
        import numpy as np
        C = 256
        H8 = 8
        DH = C // H8
        PS = 14
        CS = 3
        IMG = 168
        B = 4

        def _ln(x, g, b):
            mu = jnp.mean(x, axis=-1, keepdims=True)
            xc = x - mu
            var = jnp.mean(xc * xc, axis=-1, keepdims=True)
            return xc * jax.lax.rsqrt(var + 1e-05) * g + b

        def _forward(pixel_values, conv_w, class_emb, la_ln_q_g, la_ln_q_b, la_wq, la_ln_kv_g, la_ln_kv_b, la_wkv, la_proj_w, la_proj_b, ga_ln_q_g, ga_ln_q_b, ga_wq, ga_ln_kv_g, ga_ln_kv_b, ga_wkv, ga_proj_w, ga_proj_b, mod_w, mod_b):
            b = pixel_values.shape[0]
            pe = jax.lax.conv_general_dilated(pixel_values, conv_w, (PS, PS), 'VALID', dimension_numbers=('NCHW', 'OIHW', 'NCHW'))
            HP = pe.shape[2]
            h = HP // CS
            hw, N = (h * h, CS * CS)
            scale = C ** (-0.5)
            grid = pe.reshape(b, C, h, CS, h, CS)
            red = grid.mean(axis=(3, 5)).reshape(b, C, hw).transpose(0, 2, 1)
            win = grid.transpose(0, 2, 4, 3, 5, 1).reshape(b, hw, N, C)
            q = _ln(red, la_ln_q_g, la_ln_q_b) @ la_wq
            q = q.reshape(b, hw, H8, DH).transpose(0, 2, 1, 3)
            kv = _ln(win, la_ln_kv_g, la_ln_kv_b) @ la_wkv
            kv = kv.reshape(b, hw, N, 2, H8, DH).transpose(3, 0, 4, 1, 2, 5)
            k_, v_ = (kv[0], kv[1])
            attn = jax.nn.softmax(jnp.einsum('bhnd,bhnkd->bhnk', q * scale, k_), axis=-1)
            agg = jnp.einsum('bhnk,bhnkd->bhnd', attn, v_)
            agg = agg.transpose(0, 2, 1, 3).reshape(b, hw, C)
            local_out = red + agg @ la_proj_w + la_proj_b
            cls = jnp.broadcast_to(class_emb, (b, 1, C))
            gq = (_ln(cls, ga_ln_q_g, ga_ln_q_b) @ ga_wq).reshape(b, H8, DH)
            gkv = _ln(local_out, ga_ln_kv_g, ga_ln_kv_b) @ ga_wkv
            gkv = gkv.reshape(b, hw, 2, H8, DH).transpose(2, 0, 3, 1, 4)
            gk, gv = (gkv[0], gkv[1])
            gattn = jax.nn.softmax(jnp.einsum('bhd,bhnd->bhn', gq * scale, gk), axis=-1)
            gagg = jnp.einsum('bhn,bhnd->bhd', gattn, gv).reshape(b, 1, C)
            cls_out = cls + gagg @ ga_proj_w + ga_proj_b
            patch_out = local_out @ mod_w + mod_b
            return jnp.concatenate([patch_out, cls_out], axis=1)
        key = jax.random.key(seed)
        ks = jax.random.split(key, 16)
        nrm = lambda k, shape: jax.random.normal(k, shape, jnp.float32) * 0.02
        return {'pixel_values': jax.random.normal(ks[0], (B, 3, IMG, IMG), jnp.float32), 'pixel_masks': jnp.ones((B, 1, IMG, IMG), jnp.float32), 'conv_w': nrm(ks[1], (C, 3, PS, PS)), 'class_emb': nrm(ks[2], (C,)), 'la_ln_q_g': jnp.ones((C,)), 'la_ln_q_b': jnp.zeros((C,)), 'la_wq': nrm(ks[3], (C, C)), 'la_ln_kv_g': jnp.ones((C,)), 'la_ln_kv_b': jnp.zeros((C,)), 'la_wkv': nrm(ks[4], (C, 2 * C)), 'la_proj_w': nrm(ks[5], (C, C)), 'la_proj_b': jnp.zeros((C,)), 'ga_ln_q_g': jnp.ones((C,)), 'ga_ln_q_b': jnp.zeros((C,)), 'ga_wq': nrm(ks[6], (C, C)), 'ga_ln_kv_g': jnp.ones((C,)), 'ga_ln_kv_b': jnp.zeros((C,)), 'ga_wkv': nrm(ks[7], (C, 2 * C)), 'ga_proj_w': nrm(ks[8], (C, C)), 'ga_proj_b': jnp.zeros((C,)), 'mod_w': nrm(ks[9], (C, C)), 'mod_b': jnp.zeros((C,))}
    _L0_tok_all = _L0_tok_setup()
    _L0_tok_in = {k: v for k, v in _L0_tok_all.items() if k in ('pixel_masks', 'conv_w', 'class_emb', 'la_ln_q_g', 'la_ln_q_b', 'la_wq', 'la_ln_kv_g', 'la_ln_kv_b', 'la_wkv', 'la_proj_w', 'la_proj_b', 'ga_ln_q_g', 'ga_ln_q_b', 'ga_wq', 'ga_ln_kv_g', 'ga_ln_kv_b', 'ga_wkv', 'ga_proj_w', 'ga_proj_b', 'mod_w', 'mod_b')}
    del _L0_tok_all

    def _L0_attn_setup():
        import jax, jax.numpy as jnp
        import numpy as np
        L = 2
        D = 256
        H = 8
        DK = D // H
        DV = D // H
        T = 512
        B = 4
        INTER = 704
        EPS = 1e-06

        def rmsnorm(x, w):
            return x * jax.lax.rsqrt(jnp.mean(x * x, axis=-1, keepdims=True) + EPS) * w

        def l2norm(x):
            return x * jax.lax.rsqrt(jnp.sum(x * x, axis=-1, keepdims=True) + EPS)

        def delta_attn(x, Wq, Wk, Wv, Wb, Wo, onorm_w):
            b, t, _ = x.shape
            q = jax.nn.silu((x @ Wq).reshape(b, t, H, DK))
            k = jax.nn.silu((x @ Wk).reshape(b, t, H, DK))
            q = l2norm(q)
            k = l2norm(k)
            v = jax.nn.silu((x @ Wv).reshape(b, t, H, DV))
            beta = jax.nn.sigmoid(x @ Wb) * 2.0
            qt = q.transpose(1, 0, 2, 3)
            kt = k.transpose(1, 0, 2, 3)
            vt = v.transpose(1, 0, 2, 3)
            bt = beta.transpose(1, 0, 2)

            def step(S, inps):
                qi, ki, vi, bi = inps
                pred = jnp.einsum('bhkv,bhk->bhv', S, ki)
                S = S + bi[..., None, None] * ki[..., :, None] * (vi - pred)[..., None, :]
                o = jnp.einsum('bhkv,bhk->bhv', S, qi)
                return (S, o)
            S0 = jnp.zeros((b, H, DK, DV), x.dtype)
            _, o = jax.lax.scan(step, S0, (qt, kt, vt, bt))
            o = rmsnorm(o, onorm_w)
            o = o.transpose(1, 0, 2, 3).reshape(b, t, H * DV)
            return o @ Wo
        key = jax.random.key(seed)
        ks = jax.random.split(key, 13)
        s = 0.02
        f32 = jnp.float32
        return {'input_embeds': jax.random.normal(ks[0], (T, B, D), f32), 'Wq': jax.random.normal(ks[1], (L, D, D), f32) * s, 'Wk': jax.random.normal(ks[2], (L, D, D), f32) * s, 'Wv': jax.random.normal(ks[3], (L, D, D), f32) * s, 'Wb': jax.random.normal(ks[4], (L, D, H), f32) * s, 'Wo': jax.random.normal(ks[5], (L, D, D), f32) * s, 'onorm_w': jnp.ones((L, DV), f32) + jax.random.normal(ks[6], (L, DV), f32) * 0.02, 'norm1_w': jnp.ones((L, D), f32) + jax.random.normal(ks[7], (L, D), f32) * 0.02, 'norm2_w': jnp.ones((L, D), f32) + jax.random.normal(ks[8], (L, D), f32) * 0.02, 'Wg': jax.random.normal(ks[9], (L, D, 2 * INTER), f32) * s, 'Wd': jax.random.normal(ks[10], (L, INTER, D), f32) * s, 'final_norm_w': jnp.ones((D,), f32) + jax.random.normal(ks[11], (D,), f32) * 0.02}
    _L0_attn_all = _L0_attn_setup()
    _L0_attn_in = {k: v for k, v in _L0_attn_all.items() if k in ('Wq', 'Wk', 'Wv', 'Wb', 'Wo', 'onorm_w', 'norm1_w', 'norm2_w', 'Wg', 'Wd', 'final_norm_w')}
    del _L0_attn_all

    def _L0_ffn_setup():
        import jax, jax.numpy as jnp
        import numpy as np
        BLOCK = 16
        _GRID = jnp.array([0.0, 0.5, 1.0, 1.5, 2.0, 3.0, 4.0, 6.0], dtype=jnp.float32)
        _MID = jnp.array([0.25, 0.75, 1.25, 1.75, 2.5, 3.5, 5.0], dtype=jnp.float32)

        def fp4_quant_dequant(x):
            shape = x.shape
            xb = x.reshape(shape[:-1] + (shape[-1] // BLOCK, BLOCK))
            scale = jnp.max(jnp.abs(xb), axis=-1, keepdims=True) / 6.0
            scale = jnp.maximum(scale, jnp.float32(1e-12))
            xn = xb / scale
            idx = jnp.searchsorted(_MID, jnp.abs(xn))
            q = _GRID[idx] * jnp.sign(xn) * scale
            return q.reshape(shape)

        def fp4_linear(x, w):
            xq = fp4_quant_dequant(x)
            wq = fp4_quant_dequant(w)
            return jnp.einsum('bsk,nk->bsn', xq, wq)
        key = jax.random.key(seed)
        k1, k2, k3, k4 = jax.random.split(key, 4)
        H, I = (256, 704)
        x = jax.random.normal(k1, (4, 1024, H), dtype=jnp.float32)
        w_gate = jax.random.normal(k2, (I, H), dtype=jnp.float32) * 0.02
        w_up = jax.random.normal(k3, (I, H), dtype=jnp.float32) * 0.02
        w_down = jax.random.normal(k4, (H, I), dtype=jnp.float32) * 0.02
        return {'x': x, 'w_gate': w_gate, 'w_up': w_up, 'w_down': w_down}
    _L0_ffn_all = _L0_ffn_setup()
    _L0_ffn_in = {k: v for k, v in _L0_ffn_all.items() if k in ('w_gate', 'w_up', 'w_down')}
    del _L0_ffn_all
    return {'x': x, 'L0_tok_pixel_masks': _L0_tok_in['pixel_masks'], 'L0_tok_conv_w': _L0_tok_in['conv_w'], 'L0_tok_class_emb': _L0_tok_in['class_emb'], 'L0_tok_la_ln_q_g': _L0_tok_in['la_ln_q_g'], 'L0_tok_la_ln_q_b': _L0_tok_in['la_ln_q_b'], 'L0_tok_la_wq': _L0_tok_in['la_wq'], 'L0_tok_la_ln_kv_g': _L0_tok_in['la_ln_kv_g'], 'L0_tok_la_ln_kv_b': _L0_tok_in['la_ln_kv_b'], 'L0_tok_la_wkv': _L0_tok_in['la_wkv'], 'L0_tok_la_proj_w': _L0_tok_in['la_proj_w'], 'L0_tok_la_proj_b': _L0_tok_in['la_proj_b'], 'L0_tok_ga_ln_q_g': _L0_tok_in['ga_ln_q_g'], 'L0_tok_ga_ln_q_b': _L0_tok_in['ga_ln_q_b'], 'L0_tok_ga_wq': _L0_tok_in['ga_wq'], 'L0_tok_ga_ln_kv_g': _L0_tok_in['ga_ln_kv_g'], 'L0_tok_ga_ln_kv_b': _L0_tok_in['ga_ln_kv_b'], 'L0_tok_ga_wkv': _L0_tok_in['ga_wkv'], 'L0_tok_ga_proj_w': _L0_tok_in['ga_proj_w'], 'L0_tok_ga_proj_b': _L0_tok_in['ga_proj_b'], 'L0_tok_mod_w': _L0_tok_in['mod_w'], 'L0_tok_mod_b': _L0_tok_in['mod_b'], 'L0_attn_Wq': _L0_attn_in['Wq'], 'L0_attn_Wk': _L0_attn_in['Wk'], 'L0_attn_Wv': _L0_attn_in['Wv'], 'L0_attn_Wb': _L0_attn_in['Wb'], 'L0_attn_Wo': _L0_attn_in['Wo'], 'L0_attn_onorm_w': _L0_attn_in['onorm_w'], 'L0_attn_norm1_w': _L0_attn_in['norm1_w'], 'L0_attn_norm2_w': _L0_attn_in['norm2_w'], 'L0_attn_Wg': _L0_attn_in['Wg'], 'L0_attn_Wd': _L0_attn_in['Wd'], 'L0_attn_final_norm_w': _L0_attn_in['final_norm_w'], 'L0_ffn_w_gate': _L0_ffn_in['w_gate'], 'L0_ffn_w_up': _L0_ffn_in['w_up'], 'L0_ffn_w_down': _L0_ffn_in['w_down']}

def reference(x, L0_tok_pixel_masks, L0_tok_conv_w, L0_tok_class_emb, L0_tok_la_ln_q_g, L0_tok_la_ln_q_b, L0_tok_la_wq, L0_tok_la_ln_kv_g, L0_tok_la_ln_kv_b, L0_tok_la_wkv, L0_tok_la_proj_w, L0_tok_la_proj_b, L0_tok_ga_ln_q_g, L0_tok_ga_ln_q_b, L0_tok_ga_wq, L0_tok_ga_ln_kv_g, L0_tok_ga_ln_kv_b, L0_tok_ga_wkv, L0_tok_ga_proj_w, L0_tok_ga_proj_b, L0_tok_mod_w, L0_tok_mod_b, L0_attn_Wq, L0_attn_Wk, L0_attn_Wv, L0_attn_Wb, L0_attn_Wo, L0_attn_onorm_w, L0_attn_norm1_w, L0_attn_norm2_w, L0_attn_Wg, L0_attn_Wd, L0_attn_final_norm_w, L0_ffn_w_gate, L0_ffn_w_up, L0_ffn_w_down):
    import jax
    import jax.numpy as jnp

    def _L0_tok_ref(pixel_values, pixel_masks, conv_w, class_emb, la_ln_q_g, la_ln_q_b, la_wq, la_ln_kv_g, la_ln_kv_b, la_wkv, la_proj_w, la_proj_b, ga_ln_q_g, ga_ln_q_b, ga_wq, ga_ln_kv_g, ga_ln_kv_b, ga_wkv, ga_proj_w, ga_proj_b, mod_w, mod_b):
        import jax, jax.numpy as jnp
        import numpy as np
        C = 256
        H8 = 8
        DH = C // H8
        PS = 14
        CS = 3
        IMG = 168
        B = 4

        def _ln(x, g, b):
            mu = jnp.mean(x, axis=-1, keepdims=True)
            xc = x - mu
            var = jnp.mean(xc * xc, axis=-1, keepdims=True)
            return xc * jax.lax.rsqrt(var + 1e-05) * g + b

        def _forward(pixel_values, conv_w, class_emb, la_ln_q_g, la_ln_q_b, la_wq, la_ln_kv_g, la_ln_kv_b, la_wkv, la_proj_w, la_proj_b, ga_ln_q_g, ga_ln_q_b, ga_wq, ga_ln_kv_g, ga_ln_kv_b, ga_wkv, ga_proj_w, ga_proj_b, mod_w, mod_b):
            b = pixel_values.shape[0]
            pe = jax.lax.conv_general_dilated(pixel_values, conv_w, (PS, PS), 'VALID', dimension_numbers=('NCHW', 'OIHW', 'NCHW'))
            HP = pe.shape[2]
            h = HP // CS
            hw, N = (h * h, CS * CS)
            scale = C ** (-0.5)
            grid = pe.reshape(b, C, h, CS, h, CS)
            red = grid.mean(axis=(3, 5)).reshape(b, C, hw).transpose(0, 2, 1)
            win = grid.transpose(0, 2, 4, 3, 5, 1).reshape(b, hw, N, C)
            q = _ln(red, la_ln_q_g, la_ln_q_b) @ la_wq
            q = q.reshape(b, hw, H8, DH).transpose(0, 2, 1, 3)
            kv = _ln(win, la_ln_kv_g, la_ln_kv_b) @ la_wkv
            kv = kv.reshape(b, hw, N, 2, H8, DH).transpose(3, 0, 4, 1, 2, 5)
            k_, v_ = (kv[0], kv[1])
            attn = jax.nn.softmax(jnp.einsum('bhnd,bhnkd->bhnk', q * scale, k_), axis=-1)
            agg = jnp.einsum('bhnk,bhnkd->bhnd', attn, v_)
            agg = agg.transpose(0, 2, 1, 3).reshape(b, hw, C)
            local_out = red + agg @ la_proj_w + la_proj_b
            cls = jnp.broadcast_to(class_emb, (b, 1, C))
            gq = (_ln(cls, ga_ln_q_g, ga_ln_q_b) @ ga_wq).reshape(b, H8, DH)
            gkv = _ln(local_out, ga_ln_kv_g, ga_ln_kv_b) @ ga_wkv
            gkv = gkv.reshape(b, hw, 2, H8, DH).transpose(2, 0, 3, 1, 4)
            gk, gv = (gkv[0], gkv[1])
            gattn = jax.nn.softmax(jnp.einsum('bhd,bhnd->bhn', gq * scale, gk), axis=-1)
            gagg = jnp.einsum('bhn,bhnd->bhd', gattn, gv).reshape(b, 1, C)
            cls_out = cls + gagg @ ga_proj_w + ga_proj_b
            patch_out = local_out @ mod_w + mod_b
            return jnp.concatenate([patch_out, cls_out], axis=1)
        del pixel_masks
        return _forward(pixel_values, conv_w, class_emb, la_ln_q_g, la_ln_q_b, la_wq, la_ln_kv_g, la_ln_kv_b, la_wkv, la_proj_w, la_proj_b, ga_ln_q_g, ga_ln_q_b, ga_wq, ga_ln_kv_g, ga_ln_kv_b, ga_wkv, ga_proj_w, ga_proj_b, mod_w, mod_b)

    def _L0_attn_ref(input_embeds, Wq, Wk, Wv, Wb, Wo, onorm_w, norm1_w, norm2_w, Wg, Wd, final_norm_w):
        import jax, jax.numpy as jnp
        import numpy as np
        L = 2
        D = 256
        H = 8
        DK = D // H
        DV = D // H
        T = 512
        B = 4
        INTER = 704
        EPS = 1e-06

        def rmsnorm(x, w):
            return x * jax.lax.rsqrt(jnp.mean(x * x, axis=-1, keepdims=True) + EPS) * w

        def l2norm(x):
            return x * jax.lax.rsqrt(jnp.sum(x * x, axis=-1, keepdims=True) + EPS)

        def delta_attn(x, Wq, Wk, Wv, Wb, Wo, onorm_w):
            b, t, _ = x.shape
            q = jax.nn.silu((x @ Wq).reshape(b, t, H, DK))
            k = jax.nn.silu((x @ Wk).reshape(b, t, H, DK))
            q = l2norm(q)
            k = l2norm(k)
            v = jax.nn.silu((x @ Wv).reshape(b, t, H, DV))
            beta = jax.nn.sigmoid(x @ Wb) * 2.0
            qt = q.transpose(1, 0, 2, 3)
            kt = k.transpose(1, 0, 2, 3)
            vt = v.transpose(1, 0, 2, 3)
            bt = beta.transpose(1, 0, 2)

            def step(S, inps):
                qi, ki, vi, bi = inps
                pred = jnp.einsum('bhkv,bhk->bhv', S, ki)
                S = S + bi[..., None, None] * ki[..., :, None] * (vi - pred)[..., None, :]
                o = jnp.einsum('bhkv,bhk->bhv', S, qi)
                return (S, o)
            S0 = jnp.zeros((b, H, DK, DV), x.dtype)
            _, o = jax.lax.scan(step, S0, (qt, kt, vt, bt))
            o = rmsnorm(o, onorm_w)
            o = o.transpose(1, 0, 2, 3).reshape(b, t, H * DV)
            return o @ Wo
        x = input_embeds.transpose(1, 0, 2)
        for l in range(L):
            h = rmsnorm(x, norm1_w[l])
            x = x + delta_attn(h, Wq[l], Wk[l], Wv[l], Wb[l], Wo[l], onorm_w[l])
            h = rmsnorm(x, norm2_w[l])
            gy = h @ Wg[l]
            g, y = jnp.split(gy, 2, axis=-1)
            x = x + jax.nn.silu(g) * y @ Wd[l]
        x = rmsnorm(x, final_norm_w)
        return x.transpose(1, 0, 2)

    def _L0_ffn_ref(x, w_gate, w_up, w_down):
        import jax, jax.numpy as jnp
        import numpy as np
        BLOCK = 16
        _GRID = jnp.array([0.0, 0.5, 1.0, 1.5, 2.0, 3.0, 4.0, 6.0], dtype=jnp.float32)
        _MID = jnp.array([0.25, 0.75, 1.25, 1.75, 2.5, 3.5, 5.0], dtype=jnp.float32)

        def fp4_quant_dequant(x):
            shape = x.shape
            xb = x.reshape(shape[:-1] + (shape[-1] // BLOCK, BLOCK))
            scale = jnp.max(jnp.abs(xb), axis=-1, keepdims=True) / 6.0
            scale = jnp.maximum(scale, jnp.float32(1e-12))
            xn = xb / scale
            idx = jnp.searchsorted(_MID, jnp.abs(xn))
            q = _GRID[idx] * jnp.sign(xn) * scale
            return q.reshape(shape)

        def fp4_linear(x, w):
            xq = fp4_quant_dequant(x)
            wq = fp4_quant_dequant(w)
            return jnp.einsum('bsk,nk->bsn', xq, wq)
        gate = fp4_linear(x, w_gate)
        y = fp4_linear(x, w_up)
        h = jax.nn.silu(gate) * y
        return fp4_linear(h, w_down)
    h = _L0_tok_ref(x, L0_tok_pixel_masks, L0_tok_conv_w, L0_tok_class_emb, L0_tok_la_ln_q_g, L0_tok_la_ln_q_b, L0_tok_la_wq, L0_tok_la_ln_kv_g, L0_tok_la_ln_kv_b, L0_tok_la_wkv, L0_tok_la_proj_w, L0_tok_la_proj_b, L0_tok_ga_ln_q_g, L0_tok_ga_ln_q_b, L0_tok_ga_wq, L0_tok_ga_ln_kv_g, L0_tok_ga_ln_kv_b, L0_tok_ga_wkv, L0_tok_ga_proj_w, L0_tok_ga_proj_b, L0_tok_mod_w, L0_tok_mod_b)
    h = h + _L0_attn_ref(_layernorm(h, axis=-1), L0_attn_Wq, L0_attn_Wk, L0_attn_Wv, L0_attn_Wb, L0_attn_Wo, L0_attn_onorm_w, L0_attn_norm1_w, L0_attn_norm2_w, L0_attn_Wg, L0_attn_Wd, L0_attn_final_norm_w)
    h = h + _L0_ffn_ref(_layernorm(h, axis=-1), L0_ffn_w_gate, L0_ffn_w_up, L0_ffn_w_down)
    return h

_drawn_inputs = setup_inputs


def setup_inputs(seed=0):
    import zlib

    import numpy as np

    out = dict(_drawn_inputs(seed))
    spreads = {'L0_tok_pixel_masks': (1.0, 0.2),
     'L0_tok_la_ln_q_g': (1.0, 0.6),
     'L0_tok_la_ln_q_b': (0.0, 0.8),
     'L0_tok_la_ln_kv_g': (1.0, 0.2),
     'L0_tok_la_ln_kv_b': (0.0, 0.1),
     'L0_tok_la_proj_b': (0.0, 0.1),
     'L0_tok_ga_ln_q_g': (1.0, 0.6),
     'L0_tok_ga_ln_q_b': (0.0, 0.8),
     'L0_tok_ga_ln_kv_g': (1.0, 0.2),
     'L0_tok_ga_ln_kv_b': (0.0, 0.1),
     'L0_tok_ga_proj_b': (0.0, 0.1),
     'L0_tok_mod_b': (0.0, 0.1)}
    factors = {'L0_tok_la_wq': 8.0,
     'L0_tok_ga_wq': 7.408,
     'L0_attn_onorm_w': 6.23,
     'L0_attn_norm1_w': 3.474,
     'L0_attn_norm2_w': 8.0,
     'L0_attn_final_norm_w': 8.816,
     'L0_ffn_w_gate': 6.115,
     'L0_ffn_w_up': 6.178,
     'L0_ffn_w_down': 6.08}
    for name, (base, spread) in spreads.items():
        noise = np.random.default_rng([zlib.crc32(name.encode()), seed]).standard_normal(out[name].shape)
        drawn = base * np.exp(spread * noise) if base else spread * noise
        out[name] = jnp.asarray(drawn.astype(out[name].dtype))
    for name, factor in factors.items():
        out[name] = (out[name] * factor).astype(out[name].dtype)
    return out
```

```python
from contextlib import ExitStack

import concourse.bass as bass
from concourse import mybir

ALU = mybir.AluOpType
ACT = mybir.ActivationFunctionType
AX = mybir.AxisListType
F32 = mybir.dt.float32
I32 = mybir.dt.int32

P = 128
C = 256
CH = C // P
H = 8
DH = C // H
HP = P // DH
IMGS = 64
SLOTS = 5
NT = IMGS * SLOTS
NW = 4 * IMGS
NP_ = 9
KC, KP = 5, 118
GRP = 3 * P
LAYERS = 2
INTER = 704
FC = 6
HALVES = 2
NG = 20
PJ = 5
NB = NG // 2
EPS_LN, EPS_RMS = 1e-5, 1e-6
SCALE = C ** -0.5

(V_CLS, V_LQG, V_LQB, V_LKG, V_LKB, V_LPB, V_GQG, V_GQB, V_GKG, V_GKB, V_GPB, V_MB, V_N1, V_N2, V_FW,
 V_ON) = (0, 2, 4, 6, 8, 10, 12, 14, 16, 18, 20, 22, 24, 28, 32, 34)
NVEC = 36
T_KV, T_Q, T_PR, T_GQ, T_GKV, T_GP, T_MOD = 0, 1024, 1536, 2048, 2560, 3584, 4096
NTW = 4608
L_Q, L_K, L_VB, L_B, L_O, L_G, L_D = 0, 512, 1024, 1552, 1568, 2080, 4896
NLW = 6432
K_ID, K_BLK, K_AP, K_IC, K_LV = 0, 128, 256, 384, 416
NK = 576
LEVELS = 5
NBW = INTER // 16

ROUND_HALF, ROUND_ONE, ROUND_TWO = 1.5 * 2 ** 22, 1.5 * 2 ** 23, 1.5 * 2 ** 24
TIE_DOWN = 1.0 - 2.0 ** -22


def build(nc, xp, cw_d, vec_d, wt_d, wl_d, wf_d, cst_d, out):
    ctx = ExitStack()
    with ctx:
        def sb(name, shape, dt=F32):
            return ctx.enter_context(nc.sbuf_tensor(name, shape, dt))

        class Names:
            pass

        vec = sb("vec", [P, NVEC])
        cst = sb("cst", [P, NK])
        cwb = sb("cwb", [P, 2 * KC * C])
        cmean = sb("cmean", [KP, KC])
        wt = sb("wt", [P, NTW])
        wkvg = sb("wkvg", [P, CH, 2 * C])
        wl = sb("wl", [P, NLW])
        wf = sb("wf", [P, 6 * INTER])
        wguT = sb("wguT", [P, CH, 2 * INTER])
        wdT = sb("wdT", [P, FC, C])
        ones = sb("ones", [P, P])
        big = sb("big", [P, 6 * KC * GRP])
        pecT = sb("pecT", [P, CH, 18 * P])
        sq = sb("sq", [P, CH, 9 * P])
        xs = sb("xs", [KP, HALVES, KC, P])
        redT = sb("redT", [P, CH, NW])
        redc = sb("redc", [P, CH, P])
        redq = sb("redq", [P, CH, P])
        rsr = sb("rsr", [P, P])
        lnq = sb("lnq", [P, CH, P])
        q_sb = sb("q_sb", [P, HALVES, C])
        kvb = sb("kvb", [P, 2 * C])
        prod = sb("prod", [P, 2, C])
        sc = sb("sc", [P, HALVES, NP_, H])
        qkb = sb("qkb", [P, HALVES, H])
        rk = sb("rk", [P, HALVES, NP_])
        mx = sb("mx", [P, H])
        sm = sb("sm", [P, H])
        agg = sb("agg", [P, C])
        aggT = sb("aggT", [P, CH, P])
        locT = sb("locT", [P, CH, NW])
        clsv = sb("clsv", [P, 16])
        u = sb("u", [P, CH, H])
        gmx = sb("gmx", [P, CH, IMGS])
        gsum = sb("gsum", [P, CH, IMGS])
        gag = sb("gag", [P, CH, IMGS])
        hT0 = sb("hT0", [P, CH, NT])
        xT = sb("xT", [P, CH, NT])

        cw = cwb[0:KP, 0:KC * C].rearrange("p (k n) -> p k n", k=KC)
        cwc = cwb[0:KP, KC * C:].rearrange("p (k n) -> p k n", k=KC)
        hT = cwb[:, 0:640].rearrange("p (j n) -> p j n", j=CH)
        sqx = cwb[:, 640:1280].rearrange("p (j n) -> p j n", j=CH)
        sg = cwb[:, 1280:1920].rearrange("p (j n) -> p j n", j=CH)
        rs = cwb[:, 1920:1920 + NT]
        xg = big[0:KP, :].rearrange("p (g k n) -> p g k n", g=6, k=KC)
        apm = big[:, 0:NG * P].rearrange("p (g n) -> p g n", g=NG)
        ttc = big[:, NG * P:NG * (P + 32)].rearrange("p (g n) -> p g n", g=NG)
        qf = sq[:, :, :].rearrange("p a b -> p (a b)")
        ge = qf[:, 0:512].rearrange("p (j w t) -> p j w t", j=CH, w=4)
        rsg = qf[:, 512:512 + NW]
        wbx = qf[:, 768:1280].rearrange("p (c h d) -> p c h d", c=CH, h=H)
        ux = big[:, 4608:5120].rearrange("p (c h d) -> p c h d", c=CH, h=H)
        v_sb = big[:, 0:HALVES * NP_ * C].rearrange("p (a n c) -> p a n c", a=HALVES, n=NP_)
        lga = big[:, 10240:10752].rearrange("p (j n) -> p j n", j=CH)
        lga2 = big[:, 10880:11392].rearrange("p (j n) -> p j n", j=CH)
        oT = big[:, 10240:10880].rearrange("p (j n) -> p j n", j=CH)
        pf = pecT[:, :, :].rearrange("p a b -> p (a b)")
        skq = pf[:, 0:1280].rearrange("p (a j n) -> p a j n", a=2, j=CH)
        kqsq = pf[:, 1280:2560].rearrange("p (a j n) -> p a j n", a=2, j=CH)
        rkq = pf[:, 2560:3840].rearrange("p (a j n) -> p a j n", a=2, j=CH)
        bt = pf[:, 3840:4480].rearrange("p (j n) -> p j n", j=CH)
        sf = wf[:, :]
        kh = sf[:, 0:640].rearrange("p (j n) -> p j n", j=CH)
        kbq = sf[:, 640:1920].rearrange("p (a j n) -> p a j n", a=2, j=CH)
        act = sf[:, 1920:3840].rearrange("p (i n) -> p i n", i=FC)
        vf = wt[:, :]
        vs = vf[:, 0:640].rearrange("p (g n) -> p g n", g=NG)
        tb = vf[:, 640:660]
        bv = vf[:, 704:1344].rearrange("p (g n) -> p g n", g=NG)
        tc_ = vf[:, 1344:1984].rearrange("p (g n) -> p g n", g=NG)
        yc = vf[:, 1984:2624].rearrange("p (g n) -> p g n", g=NG)
        uc = vf[:, 2624:3264].rearrange("p (g n) -> p g n", g=NG)
        osb = vf[:, 3264:3904].rearrange("p (g n) -> p g n", g=NG)
        osq = vf[:, 3904:4544].rearrange("p (g n) -> p g n", g=NG)
        oss = sb("oss", [P, NG])
        h1 = sb("h1", [P, 3, C])
        xn = pf[:, 0:3 * C].rearrange("p (t n) -> p t n", t=3)
        stt = sb("stt", [P, 3, 6])
        mv = sb("mv", [P, 3, 2])
        rs3 = sb("rs3", [P, 3])
        xqT = pf[:, 3 * C:3 * C + CH * NT].rearrange("p (c n) -> p c n", c=CH)
        hh = big[:, 0:3 * INTER].rearrange("p (t n) -> p t n", t=3)
        sgu = big[:, 3 * INTER:4 * INTER]
        hqT = big[:, 3072:3072 + FC * NT].rearrange("p (i n) -> p i n", i=FC)
        qa = sb("qa", [P, 3, 48 * 16])
        qs = sb("qs", [P, 4, 48])

        ps = ctx.enter_context(nc.psum_tensor("ps", [P, 8, 512], F32))

        def bank32(b, r):
            return ps[r, b, 0:NT].rearrange("p (g n) -> p g n", n=32)

        def both(x, q):
            return x[32 * q:32 * q + 32, :, :].rearrange("p (a g) n -> p a (g n)", a=2)

        ident = cst[:, K_ID:K_ID + P]
        blk = cst[:, K_BLK:K_BLK + P]
        map_ = cst[:, K_AP:K_AP + P]
        ic = cst[:, K_IC:K_IC + 32]
        wkv = wt[:, T_KV:T_KV + 1024].rearrange("p (c n) -> p c n", c=CH)
        gwkv = wt[:, T_GKV:T_GKV + 1024].rearrange("p (c n) -> p c n", c=CH)

        def tw(at):
            return wt[:, at:at + 512].rearrange("p (c n) -> p c n", c=CH)

        def lw(at, n=C, c=CH):
            return wl[:, at:at + c * n].rearrange("p (c n) -> p c n", c=c)

        wvb = wl[:, L_VB:L_VB + 528].rearrange("p (c j n) -> p c j n", c=CH, j=2)
        wb = lw(L_B, H)
        wg = lw(L_G, 2 * INTER)
        wd = lw(L_D, C, FC)

        once = """cw vecs consts tokw ffnw cwc wkvg ones conv copied squared xsum red_mm red mean_mm centered
            csq var_mm rstd lnq q_mm q kv_mm k_used v_kept stat_mm rk score softmax attn vprod agg aggr_t aggT
            proj_mm loc kvb_mm kvb cls_mm cls_c cls_v cls_n gq_mm u ga_mean ga_c ga_sq ga_var ga_rs ga_n ga_s ga_max
            ga_e ga_sum ga_gv ga_agg ga_proj h0 mod_mm x_mean x_c x_sq x_var x_rs wq wq_t wqT
            zeros fin_sq fin_ms fin_rs fin_y h1_t h1 stats rs3 xn xq xq_t xqT gu_mm gate hh hq hq_t hqT
            out_mm outs stored"""
        EACH = {
            "lwa": 16, "lwb": 16, "x": 4, "n_sq": 2, "n_ms": 2, "n_rs": 4, "h": 4, "k_mm": 1, "q2_mm": 1, "bt_mm": 1,
            "v_mm": 1, "silu": 10, "ss_mm": 2, "rkq": 4, "kq": 5, "wbx": 1, "ap_mm": 3, "ap": 3, "y_mm": 2 * LEVELS, "y": 2 * (LEVELS - 1),
            "z_mm": 2 * (LEVELS - 1), "t": 4 * LEVELS, "u1_mm": 2, "u1": 1, "u1_two": 1, "r_mm": 2, "b2": 2, "u2_mm": 2, "u2": 1, "u2_two": 1,
            "o_mm": 1, "osq": 1, "oss": 1, "ors": 2, "on": 1, "o_t": 1, "oT": 3, "wo_mm": 2, "up_mm": FC, "sg": FC,
            "act": FC, "dn_mm": 2,
        }
        S = {n: ctx.enter_context(nc.semaphore("s_" + n)) for n in (*once.split(), *EACH)}
        s_x = [ctx.enter_context(nc.semaphore(f"s_patches{g}")) for g in range(6)]
        s_dq = ctx.enter_context(nc.semaphore("s_quant_step"))

        blk_ = ctx.enter_context(nc.Block())

        def load_layer(sp, l, what):
            if what == 0:
                sp.dma_start(wl[:, 0:L_G], wl_d[l, :, 0:L_G]).then_inc(S["lwa"], 16)
            else:
                sp.dma_start(wl[:, L_G:NLW], wl_d[l, :, L_G:NLW]).then_inc(S["lwb"], 16)

        @blk_.sync
        def _(sp):
            sp.dma_start(cw[:, :, :], cw_d).then_inc(S["cw"], 16)
            sp.dma_start(xg[:, 0], xp[0]).then_inc(s_x[0], 16)
            sp.dma_start(vec[:, :], vec_d).then_inc(S["vecs"], 16)
            sp.dma_start(cst[:, :], cst_d).then_inc(S["consts"], 16)
            sp.dma_start(xg[:, 1], xp[1]).then_inc(s_x[1], 16)
            sp.dma_start(wt[:, :], wt_d).then_inc(S["tokw"], 16)
            for g in range(2, 4):
                sp.dma_start(xg[:, g], xp[g]).then_inc(s_x[g], 16)
            sp.dma_start(wf[:, :], wf_d).then_inc(S["ffnw"], 16)
            for g in range(4, 6):
                sp.dma_start(xg[:, g], xp[g]).then_inc(s_x[g], 16)
            load_layer(sp, 0, 0)
            load_layer(sp, 0, 1)
            for l in range(1, LAYERS):
                sp.wait_ge(S["wo_mm"], EACH["wo_mm"] * (l - 1) + 2)
                load_layer(sp, l, 0)
                sp.wait_ge(S["dn_mm"], EACH["dn_mm"] * (l - 1) + 2)
                load_layer(sp, l, 1)
            o_v = out.rearrange("t s c -> s t c")
            for p in range(3):
                sp.wait_ge(S["outs"], p + 1)
                for a in range(2 if p < 2 else 1):
                    sp.dma_start(o_v[2 * p + a], h1[64 * a:64 * a + 64, p, :]).then_inc(S["stored"], 16)
            sp.wait_ge(S["stored"], 16 * SLOTS)

        @blk_.gpsimd
        def _(pool):
            nc.gpsimd.memset(ones[:, :], 1.0 / C).then_inc(S["ones"], 1)
            nc.gpsimd.memset(h1[:, 2, :], 0.0).then_inc(S["zeros"], 1)
            n = 0
            for g in range(6):
                pool.wait_ge(s_x[g], 16)
                hf = g // 3
                for a in range(3):
                    new = xg[:, g, :, a * P:(a + 1) * P]
                    if g % 3 == 0 and a == 0:
                        continue
                    old = xg[:, g, :, 0:P] if (g % 3 == 0 and a == 1) else xs[:, hf]
                    if n and not (g % 3 == 0 and a == 1):
                        pool.wait_ge(S["xsum"], n)
                    nc.gpsimd.tensor_tensor(xs[:, hf], old, new, ALU.add).then_inc(S["xsum"], 1)
                    n += 1
            pool.wait_ge(S["attn"], 1)
            pool.wait_ge(S["v_kept"], 5)
            v0 = v_sb[:, 0].rearrange("p n (h d) -> p (n h) d", h=H)
            w0 = sc[:, 0].rearrange("p n h -> p (n h)").unsqueeze(2).broadcast_to([P, NP_ * H, DH])
            nc.gpsimd.tensor_tensor(v0, v0, w0, ALU.mult).then_inc(S["vprod"], 1)
            pool.wait_ge(S["wq_t"], 9)
            nc.gpsimd.memset(act[0:64, FC - 1, :], 0.0).then_inc(S["zeros"], 1)
            for l in range(LAYERS):
                pool.wait_ge(S["lwa"], EACH["lwa"] * l + 16)
                if l:
                    pool.wait_ge(S["bt_mm"], l)
                nc.gpsimd.tensor_copy(wbx[:, :, :, :].rearrange("p c h d -> p (c h) d"),
                                      wb.rearrange("p c h -> p (c h)").unsqueeze(2).broadcast_to([P, CH * H, DH])
                                      ).then_inc(S["wbx"], 1)

        def rsqrt(act_, out_, in_, sem, eps, scale=1.0, k=None, layer=None):
            nc.scalar.activation(out_, in_, ACT.Ln, bias=eps, scale=scale).then_inc(S[sem], 1)
            act_.wait_ge(S[sem], k if layer is None else EACH[sem] * layer + k)
            nc.scalar.activation(out_, out_, ACT.Exp, scale=-0.5).then_inc(S[sem], 1)

        @blk_.scalar
        def _(act_):
            nc.scalar.preload_act_table_set("natural_log_exp_and_others")

            def square_group(g):
                if g == 3:
                    act_.wait_ge(S["stat_mm"], 1)
                for c in range(CH):
                    act_.wait_ge(S["copied"], 2 * g + c + 1)
                    nc.scalar.activation(sq[:, c, g % 3 * GRP:(g % 3 + 1) * GRP], pecT[:, c, g * GRP:(g + 1) * GRP],
                                         ACT.Square).then_inc(S["squared"], 1)

            square_group(0)
            act_.wait_ge(S["cls_c"], 1)
            nc.scalar.activation(clsv[:, 2:4], clsv[:, 0:2], ACT.Square).then_inc(S["cls_v"], 1)
            square_group(1)
            act_.wait_ge(S["cls_mm"], 2)
            rsqrt(act_, clsv[:, 4:5], ps[:, 7, 8:9], "cls_v", EPS_LN, k=2)
            act_.wait_ge(S["kvb_mm"], 1)
            nc.scalar.copy(kvb[:, :], ps[:, 6, :]).then_inc(S["kvb"], 1)
            square_group(2)
            square_group(3)

            def red_sq(hf):
                if hf:
                    act_.wait_ge(S["var_mm"], hf)
                act_.wait_ge(S["centered"], hf + 1)
                nc.scalar.activation(redq[:, :, :], redc[:, :, :], ACT.Square).then_inc(S["csq"], 1)

            def red_rs(hf):
                act_.wait_ge(S["var_mm"], hf + 1)
                if hf:
                    act_.wait_ge(S["lnq"], 4 * hf)
                rsqrt(act_, rsr[:, :], ps[:, 5, 128:256], "rstd", EPS_LN, k=2 * hf + 1)

            def q_copy(hf):
                act_.wait_ge(S["q_mm"], hf + 1)
                nc.scalar.copy(q_sb[:, hf, :], ps[:, 5, 256:512]).then_inc(S["q"], 1)

            def rk_half(hf):
                act_.wait_ge(S["stat_mm"], hf + 1)
                rsqrt(act_, rk[:, hf, :], ps[:, 7 - hf, 0:NP_], "rk", EPS_LN, k=2 * hf + 1)

            def keep_v(un):
                hf, uu = divmod(un, 5)
                n = min(2, NP_ - 2 * uu)
                act_.wait_ge(S["kv_mm"], un + 1)
                nc.scalar.copy(v_sb[:, hf, 2 * uu:2 * uu + n, :],
                               ps[:, 2 + un % 2, 0:n * C].rearrange("p (n c) -> p n c", n=n)
                               ).then_inc(S["v_kept"], 1)

            red_sq(0)
            red_rs(0)
            square_group(4)
            q_copy(0)
            square_group(5)
            rk_half(0)
            red_sq(1)
            keep_v(0)
            red_rs(1)
            keep_v(1)
            q_copy(1)
            for un in range(2, 5):
                keep_v(un)
            rk_half(1)
            act_.wait_ge(S["softmax"], 3)
            nc.scalar.activation(sc[:, 0], sc[:, 0], ACT.Exp, scale=SCALE).then_inc(S["score"], 1)
            for un in range(5, 10):
                keep_v(un)
            act_.wait_ge(S["softmax"], 8)
            nc.scalar.activation(sc[:, 1], sc[:, 1], ACT.Exp, scale=SCALE).then_inc(S["score"], 1)
            act_.wait_ge(S["ga_c"], 1)
            nc.scalar.activation(lga2[:, :, :], lga[:, :, :], ACT.Square).then_inc(S["ga_sq"], 1)
            act_.wait_ge(S["ga_var"], 1)
            rsqrt(act_, rsg, ps[:, 1, 0:NW], "ga_rs", EPS_LN, k=1)
            act_.wait_ge(S["ga_max"], 2)
            nc.scalar.activation(ge[:, :, :, :], ge[:, :, :, :], ACT.Exp, scale=SCALE).then_inc(S["ga_e"], 1)
            for i in range(9):
                act_.wait_ge(S["wq_t"], i + 1)
                b = 4 + i % 2
                if i < 6:
                    nt = min(4, 11 * 2 - 4 * i)
                    dst = wguT[:, :, :].rearrange("p c (i n) -> p i c n", i=11)[:, 2 * i:2 * i + nt // 2]
                    nc.scalar.copy(dst, ps[:, b, 0:nt * P].rearrange("p (i c n) -> p i c n", c=2, n=P)
                                   ).then_inc(S["wqT"], 1)
                elif i < 8:
                    k0 = 2 * (i - 6)
                    nc.scalar.copy(wdT[:, k0:k0 + 2, :],
                                   ps[:, b, :].rearrange("p (k n) -> p k n", k=2)).then_inc(S["wqT"], 1)
                else:
                    nc.scalar.copy(wdT[:, 4, :], ps[:, b, 0:C]).then_inc(S["wqT"], 1)
                    nc.scalar.copy(wdT[0:64, 5, :], ps[0:64, b, C:2 * C]).then_inc(S["wqT"], 1)
            act_.wait_ge(S["x_c"], 1)
            nc.scalar.activation(sqx[:, :, :], xT[:, :, :], ACT.Square).then_inc(S["x_sq"], 1)
            act_.wait_ge(S["x_var"], 1)
            rsqrt(act_, rs[:, :], ps[:, 1, 0:NT], "x_rs", EPS_LN, k=1)

            def norm(l, half):
                act_.wait_ge(S["x"], EACH["x"] * l + 2 + 2 * half)
                nc.scalar.activation(sqx[:, :, :], xT[:, :, :], ACT.Square).then_inc(S["n_sq"], 1)
                act_.wait_ge(S["n_ms"], EACH["n_ms"] * l + half + 1)
                rsqrt(act_, rs[:, :], ps[:, 0, 0:NT], "n_rs", EPS_RMS, k=2 * half + 1, layer=l)

            def layer(l):
                norm(l, 0)
                nc.scalar.preload_act_table_set("silu_and_others")
                act_.wait_ge(S["k_mm"], EACH["k_mm"] * l + 1)
                nc.scalar.activation(skq[:, 0], ps[:, 1:3, 0:NT], ACT.Silu).then_inc(S["silu"], 1)
                act_.wait_ge(S["q2_mm"], EACH["q2_mm"] * l + 1)
                nc.scalar.activation(skq[:, 1], ps[:, 3:5, 0:NT], ACT.Silu).then_inc(S["silu"], 1)
                for a in range(2):
                    act_.wait_ge(S["silu"], EACH["silu"] * l + a + 1)
                    nc.scalar.activation(kqsq[:, a], skq[:, a], ACT.Square).then_inc(S["silu"], 1)
                act_.wait_ge(S["bt_mm"], EACH["bt_mm"] * l + 1)
                nc.scalar.activation(bt[:, :, :], ps[:, 5:7, 0:NT], ACT.Tanh, scale=0.5).then_inc(S["silu"], 1)
                act_.wait_ge(S["v_mm"], EACH["v_mm"] * l + 1)
                for pj0, n, src in ((0, 2, ps[:, 7, 0:264]), (2, 2, ps[:, 0, 0:264]), (4, 1, ps[:, 7, 264:396])):
                    s = src.rearrange("p (j n) -> p j n", j=n)
                    dst = vs[:, 4 * pj0:4 * pj0 + 4 * n, :].rearrange("p (j h) d -> p j (h d)", j=n)
                    last = nc.scalar.activation(dst, s[:, :, 0:P], ACT.Silu)
                    if pj0 < 4:
                        last.then_inc(S["silu"], 1)
                    last = nc.scalar.activation(tb[:, 4 * pj0:4 * pj0 + 4 * n].rearrange("p (j h) -> p j h", j=n),
                                                s[:, :, P:P + 4], ACT.Tanh, scale=0.5)
                    last.then_inc(S["silu"], 1)
                nc.scalar.preload_act_table_set("natural_log_exp_and_others")
                for a in range(2):
                    act_.wait_ge(S["ss_mm"], EACH["ss_mm"] * l + a + 1)
                    rsqrt(act_, rkq[:, a], ps[:, 1 + 2 * a:3 + 2 * a, 0:NT], "rkq", EPS_RMS, k=2 * a + 1, layer=l)
                for lev in range(1, LEVELS):
                    for b in range(2):
                        act_.wait_ge(S["y_mm"], EACH["y_mm"] * l + 2 * lev + b + 1)
                        if lev > 1:
                            act_.wait_ge(S["z_mm"], EACH["z_mm"] * l + 2 * (lev - 2) + b + 1)
                        nc.scalar.copy(yc[:, NB * b:NB * (b + 1), :], bank32(b, slice(0, P))).then_inc(S["y"], 1)
                act_.wait_ge(S["u1_mm"], EACH["u1_mm"] * l + 1)
                nc.scalar.copy(both(uc, 0), ps[0:32, 4:6, 0:NT]).then_inc(S["u1"], 1)
                act_.wait_ge(S["u2_mm"], EACH["u2_mm"] * l + 1)
                nc.scalar.copy(both(uc, 1), ps[32:64, 4:6, 0:NT]).then_inc(S["u2"], 1)
                act_.wait_ge(S["o_mm"], EACH["o_mm"] * l + 1)
                nc.scalar.activation(osq[:, :, :].rearrange("p (a g) n -> p a (g n)", a=2), ps[:, 6:8, 0:NT],
                                     ACT.Square).then_inc(S["osq"], 1)
                act_.wait_ge(S["oss"], EACH["oss"] * l + 1)
                rsqrt(act_, oss[:, :], oss[:, :], "ors", EPS_RMS, scale=1.0 / DH, k=1, layer=l)
                norm(l, 1)
                nc.scalar.preload_act_table_set("silu_and_others")
                for i in range(FC):
                    act_.wait_ge(S["up_mm"], EACH["up_mm"] * l + i + 1)
                    if i >= 2:
                        act_.wait_ge(S["act"], EACH["act"] * l + i - 1)
                    if i < FC - 1:
                        nc.scalar.activation(sg[:, i % 2, :], ps[:, i % 3, 0:NT], ACT.Silu).then_inc(S["sg"], 1)
                    else:
                        nc.scalar.activation(sg[64:P, i % 2, :], ps[0:64, i % 3, 0:NT], ACT.Silu).then_inc(S["sg"], 1)

            for l in range(LAYERS):
                layer(l)
                nc.scalar.preload_act_table_set("natural_log_exp_and_others")

            act_.wait_ge(S["x"], EACH["x"] * LAYERS + 2)
            nc.scalar.activation(sqx[:, :, :], xT[:, :, :], ACT.Square).then_inc(S["fin_sq"], 1)
            act_.wait_ge(S["fin_ms"], 1)
            rsqrt(act_, rs[:, :], ps[:, 0, 0:NT], "fin_rs", EPS_RMS, k=1)
            act_.wait_ge(S["h1_t"], 1)
            act_.wait_ge(S["zeros"], 1)
            nc.scalar.copy(h1[:, 0:2, :], ps[:, 1, :].rearrange("p (t n) -> p t n", t=2)).then_inc(S["h1"], 1)
            nc.scalar.copy(h1[0:64, 2, :], ps[0:64, 2, 0:C]).then_inc(S["h1"], 1)
            act_.wait_ge(S["stats"], 6)
            rsqrt(act_, rs3[:, :], mv[:, :, 1], "rs3", EPS_LN, k=1)
            act_.wait_ge(S["xq_t"], 1)
            nc.scalar.copy(xqT[:, :, 0:2 * P],
                           ps[:, 3, :].rearrange("p (t c n) -> p c t n", t=2, c=2)).then_inc(S["xqT"], 1)
            nc.scalar.copy(xqT[:, :, 2 * P:NT], ps[:, 4, 0:P].rearrange("p (c n) -> p c n", c=2)).then_inc(S["xqT"], 1)
            nc.scalar.preload_act_table_set("silu_and_others")
            for p in range(3):
                n = P if p < 2 else 64
                act_.wait_ge(S["gu_mm"], p + 1)
                if p:
                    act_.wait_ge(S["hh"], p)
                b = 4 * (p % 2)
                nc.scalar.activation(sgu[0:n, :].rearrange("p (a n) -> p a n", a=2), ps[0:n, b:b + 2, 0:352],
                                     ACT.Silu).then_inc(S["gate"], 1)
            for p in range(3):
                n = P if p < 2 else 64
                act_.wait_ge(S["hq_t"], p + 1)
                nc.scalar.copy(hqT[:, 0:4, P * p:P * p + n],
                               ps[:, 2 * p, 0:4 * n].rearrange("p (k n) -> p k n", k=4)).then_inc(S["hqT"], 1)
                nc.scalar.copy(hqT[:, 4, P * p:P * p + n], ps[:, 2 * p + 1, 0:n]).then_inc(S["hqT"], 1)
                nc.scalar.copy(hqT[0:64, 5, P * p:P * p + n], ps[0:64, 2 * p + 1, n:2 * n]).then_inc(S["hqT"], 1)

        @blk_.vector
        def _(dve):
            v = nc.vector
            steps = [0]

            def step(ins):
                steps[0] += 1
                ins.then_inc(s_dq, 1)
                dve.wait_ge(s_dq, steps[0])

            def quantize(src, nb, done):
                p = src.shape[0]
                s3 = src.rearrange("p (b n) -> p b n", n=16)
                am, scl, ri = (qs[0:p, k, 0:nb] for k in range(3))
                a, r1, r2 = (qa[0:p, k, 0:16 * nb] for k in range(3))

                def each(x):
                    return x.unsqueeze(2).broadcast_to([p, nb, 16])

                step(v.tensor_reduce(am, s3, AX.X, ALU.max, apply_absolute_value=True))
                step(v.tensor_scalar(scl, am, 1.0 / 6.0, 1e-12, ALU.mult, ALU.max))
                step(v.reciprocal(ri, scl))
                step(v.tensor_scalar(ri, ri, TIE_DOWN, None, ALU.mult))
                step(v.tensor_tensor(r1.rearrange("p (b n) -> p b n", n=16), s3, each(ri), ALU.mult))
                step(v.tensor_scalar(a.bitcast(I32), r1.bitcast(I32), 0x7FFFFFFF, None, ALU.bitwise_and))
                step(v.tensor_scalar(r2, a, 2.0, 4.0, ALU.max, ALU.min))
                v.tensor_scalar(r1, a, 2.0, ROUND_HALF, ALU.min, ALU.add)
                step(v.tensor_scalar(r2, r2, ROUND_ONE, ROUND_ONE, ALU.add, ALU.subtract))
                step(v.tensor_scalar(a, a, 4.0, ROUND_TWO, ALU.max, ALU.add))
                step(v.scalar_tensor_tensor(r2, r1, ROUND_HALF, r2, ALU.subtract, ALU.add))
                step(v.scalar_tensor_tensor(r2, a, ROUND_TWO + 6.0, r2, ALU.subtract, ALU.add))
                step(v.scalar_tensor_tensor(a.bitcast(I32), src.bitcast(I32), -0x80000000, r2.bitcast(I32),
                                            ALU.bitwise_and, ALU.bitwise_or))
                v.tensor_tensor(s3, a.rearrange("p (b n) -> p b n", n=16), each(scl), ALU.mult).then_inc(S[done], 1)
                dve.wait_ge(S[done], quantized.setdefault(done, 0) + 1)
                quantized[done] += 1

            quantized = {}

            dve.wait_ge(S["cw"], 16)
            v.tensor_reduce(cmean[:, :], cw[:, :, :], AX.X, ALU.add).then_inc(S["cwc"], 1)
            dve.wait_ge(S["cwc"], 1)
            v.tensor_scalar(cmean[:, :], cmean[:, :], 1.0 / C, None, ALU.mult).then_inc(S["cwc"], 1)
            dve.wait_ge(S["cwc"], 2)
            v.tensor_tensor(cwc[:, :, :], cw[:, :, :], cmean[:, :].unsqueeze(2).broadcast_to([KP, KC, C]),
                            ALU.subtract).then_inc(S["cwc"], 1)

            def copy_group(g):
                for c in range(CH):
                    i = 2 * g + c
                    dve.wait_ge(S["conv"], i + 1)
                    v.tensor_copy(pecT[:, c, g * GRP:(g + 1) * GRP], ps[:, i % 4, 0:GRP]).then_inc(S["copied"], 1)

            copy_group(0)
            dve.wait_ge(S["tokw"], 16)
            dve.wait_ge(S["vecs"], 16)
            for c in range(CH):
                v.tensor_scalar(wkvg[:, c, :], wkv[:, c, :], vec[:, V_LKG + c:V_LKG + c + 1], None,
                                ALU.mult).then_inc(S["wkvg"], 1)
            dve.wait_ge(S["cls_mm"], 1)
            v.tensor_scalar(clsv[:, 0:2], vec[:, V_CLS:V_CLS + 2], ps[:, 7, 0:1], None,
                            ALU.subtract).then_inc(S["cls_c"], 1)
            copy_group(1)
            dve.wait_ge(S["ffnw"], 16)
            quantize(wf[:, 0:INTER], NBW, "wq")
            copy_group(2)
            dve.wait_ge(S["cls_v"], 3)
            dve.wait_ge(S["cls_c"], 1)
            for c in range(CH):
                v.scalar_tensor_tensor(clsv[:, 6 + c:7 + c], clsv[:, c:c + 1], vec[:, V_GQG + c:V_GQG + c + 1],
                                       clsv[:, 4:5], ALU.mult, ALU.mult).then_inc(S["cls_n"], 1)
            dve.wait_ge(S["cls_n"], 2)
            v.tensor_tensor(clsv[:, 6:8], clsv[:, 6:8], vec[:, V_GQB:V_GQB + 2], ALU.add).then_inc(S["cls_n"], 1)
            quantize(wf[:, INTER:2 * INTER], NBW, "wq")
            dve.wait_ge(S["gq_mm"], 1)
            for c in range(CH):
                v.tensor_tensor(prod[:, c, :], gwkv[:, c, 0:C], ps[:, 6, 0:C], ALU.mult).then_inc(S["u"], 1)
            dve.wait_ge(S["u"], 2)
            v.tensor_reduce(u[:, :, :].rearrange("p c h -> p (c h)"),
                            prod[:, :, :].rearrange("p c (h d) -> p (c h) d", h=H), AX.X, ALU.add).then_inc(S["u"], 1)
            copy_group(3)

            def red_a(hf):
                cols = slice(hf * P, (hf + 1) * P)
                dve.wait_ge(S["red_mm"], hf + 1)
                v.tensor_scalar(redT[:, :, cols], ps[:, 4, 0:C].rearrange("p (c n) -> p c n", c=2), 1.0 / NP_, None,
                                ALU.mult).then_inc(S["red"], 1)

            def red_b(hf):
                cols = slice(hf * P, (hf + 1) * P)
                dve.wait_ge(S["mean_mm"], hf + 1)
                dve.wait_ge(S["red"], hf + 1)
                v.tensor_tensor(redc[:, :, :], redT[:, :, cols],
                                ps[:, 5, 0:P].unsqueeze(1).broadcast_to([P, CH, P]), ALU.subtract
                                ).then_inc(S["centered"], 1)

            def red_c(hf):
                dve.wait_ge(S["rstd"], 2 * hf + 2)
                dve.wait_ge(S["centered"], hf + 1)
                if hf:
                    dve.wait_ge(S["q_mm"], hf)
                for c in range(CH):
                    v.scalar_tensor_tensor(lnq[:, c, :], redc[:, c, :], vec[:, V_LQG + c:V_LQG + c + 1], rsr[:, :],
                                           ALU.mult, ALU.mult).then_inc(S["lnq"], 1)
                dve.wait_ge(S["lnq"], 4 * hf + 2)
                for c in range(CH):
                    v.tensor_scalar(lnq[:, c, :], lnq[:, c, :], vec[:, V_LQB + c:V_LQB + c + 1], None,
                                    ALU.add).then_inc(S["lnq"], 1)

            ku = [0]

            def k_signal(ins):
                ku[0] += 1
                ins.then_inc(S["k_used"], 1)

            def scores_bias(hf):
                dve.wait_ge(S["q"], hf + 1)
                dve.wait_ge(S["kvb"], 1)
                if ku[0]:
                    dve.wait_ge(S["k_used"], ku[0])
                else:
                    dve.wait_ge(S["u"], 3)
                k_signal(v.tensor_tensor(prod[:, 0, :], q_sb[:, hf, :], kvb[:, 0:C], ALU.mult))
                dve.wait_ge(S["k_used"], ku[0])
                k_signal(v.tensor_reduce(qkb[:, hf, :], prod[:, 0, :].rearrange("p (h d) -> p h d", h=H), AX.X,
                                         ALU.add))

            def scores(un):
                hf, uu = divmod(un, 5)
                n = min(2, NP_ - 2 * uu)
                dve.wait_ge(S["kv_mm"], un + 1)
                dve.wait_ge(S["k_used"], ku[0])
                v.tensor_tensor(prod[:, 0:n, :], ps[:, un % 2, 0:n * C].rearrange("p (n c) -> p n c", n=n),
                                q_sb[:, hf, :].unsqueeze(1).broadcast_to([P, n, C]), ALU.mult
                                ).then_inc(S["k_used"], 1)
                ku[0] += 1
                dve.wait_ge(S["k_used"], ku[0])
                k_signal(v.tensor_reduce(sc[:, hf, 2 * uu:2 * uu + n, :].rearrange("p n h -> p (n h)"),
                                         prod[:, 0:n, :].rearrange("p n (h d) -> p (n h) d", h=H), AX.X, ALU.add))

            def softmax_a(hf):
                def nh(x):
                    return x.unsqueeze(1).broadcast_to([P, NP_, H])
                s = sc[:, hf]
                dve.wait_ge(S["k_used"], ku[0])
                dve.wait_ge(S["rk"], 2 * hf + 2)
                v.tensor_tensor(s, s, rk[:, hf, :].unsqueeze(2).broadcast_to([P, NP_, H]), ALU.mult
                                ).then_inc(S["softmax"], 1)
                dve.wait_ge(S["softmax"], 5 * hf + 1)
                v.tensor_tensor(s, s, nh(qkb[:, hf, :]), ALU.add).then_inc(S["k_used"], 1)
                ku[0] += 1
                dve.wait_ge(S["k_used"], ku[0])
                v.tensor_reduce(mx[:, :], s.rearrange("p n h -> p h n"), AX.X, ALU.max).then_inc(S["softmax"], 1)
                dve.wait_ge(S["softmax"], 5 * hf + 2)
                v.tensor_tensor(s, s, nh(mx[:, :]), ALU.subtract).then_inc(S["softmax"], 1)

            def softmax_b(hf):
                def nh(x):
                    return x.unsqueeze(1).broadcast_to([P, NP_, H])
                s = sc[:, hf]
                dve.wait_ge(S["score"], hf + 1)
                v.tensor_reduce(sm[:, :], s.rearrange("p n h -> p h n"), AX.X, ALU.add).then_inc(S["softmax"], 1)
                dve.wait_ge(S["softmax"], 5 * hf + 4)
                v.reciprocal(sm[:, :], sm[:, :]).then_inc(S["softmax"], 1)
                dve.wait_ge(S["softmax"], 5 * hf + 5)
                k_signal(v.tensor_tensor(s, s, nh(sm[:, :]), ALU.mult))
                dve.wait_ge(S["k_used"], ku[0])
                v.tensor_tensor(s, s, rk[:, hf, :].unsqueeze(2).broadcast_to([P, NP_, H]), ALU.mult
                                ).then_inc(S["attn"], 1)

            def gather(hf):
                vv = v_sb[:, hf]
                if hf:
                    dve.wait_ge(S["attn"], 2)
                    dve.wait_ge(S["v_kept"], 10)
                    v3 = vv.rearrange("p n (h d) -> p (n h) d", h=H)
                    v.tensor_tensor(v3, v3, sc[:, hf].rearrange("p n h -> p (n h)").unsqueeze(2).broadcast_to(
                        [P, NP_ * H, DH]), ALU.mult).then_inc(S["vprod"], 1)
                dve.wait_ge(S["vprod"], hf + 1)
                if hf:
                    dve.wait_ge(S["aggr_t"], 1)
                v.tensor_reduce(agg[:, :], vv.rearrange("p n c -> p c n"), AX.X, ALU.add).then_inc(S["agg"], 1)
                dve.wait_ge(S["agg"], 2 * hf + 1)
                v.tensor_tensor(agg[:, :], agg[:, :], kvb[:, C:2 * C], ALU.add).then_inc(S["agg"], 1)

            def local(hf):
                dve.wait_ge(S["aggr_t"], hf + 1)
                if hf:
                    dve.wait_ge(S["proj_mm"], hf)
                v.tensor_copy(aggT[:, :, :], ps[:, 4, 0:C].rearrange("p (c n) -> p c n", c=2)).then_inc(S["aggT"], 1)
                dve.wait_ge(S["proj_mm"], hf + 1)
                cols = slice(hf * P, (hf + 1) * P)
                for c in range(CH):
                    v.scalar_tensor_tensor(locT[:, c, cols], ps[:, 5, c * P:(c + 1) * P],
                                           vec[:, V_LPB + c:V_LPB + c + 1], redT[:, c, cols], ALU.add, ALU.add
                                           ).then_inc(S["loc"], 1)

            red_a(0)
            red_b(0)
            quantize(wf[:, 2 * INTER:3 * INTER], NBW, "wq")
            red_c(0)
            copy_group(4)
            quantize(wf[:, 3 * INTER:4 * INTER], NBW, "wq")
            scores_bias(0)
            copy_group(5)
            red_a(1)
            scores(0)
            red_b(1)
            scores(1)
            red_c(1)
            for un in range(2, 5):
                scores(un)
            softmax_a(0)
            softmax_b(0)
            scores_bias(1)
            scores(5)
            quantize(wf[:, 4 * INTER:5 * INTER], NBW, "wq")
            scores(6)
            gather(0)
            scores(7)
            local(0)
            scores(8)
            scores(9)
            softmax_a(1)
            softmax_b(1)
            gather(1)
            local(1)
            dve.wait_ge(S["u"], 3)
            dve.wait_ge(S["red_mm"], 2)
            dve.wait_ge(S["xsum"], 16)
            v.tensor_copy(ux.rearrange("p c h d -> p (c h) d"),
                          u[:, :, :].rearrange("p c h -> p (c h)").unsqueeze(2).broadcast_to([P, CH * H, DH])
                          ).then_inc(S["u"], 1)
            dve.wait_ge(S["loc"], 4)
            dve.wait_ge(S["ga_mean"], 1)
            v.tensor_tensor(lga[:, :, :], locT[:, :, :], ps[:, 0, 0:NW].unsqueeze(1).broadcast_to([P, CH, NW]),
                            ALU.subtract).then_inc(S["ga_c"], 1)
            quantize(wf[:, 5 * INTER:6 * INTER], NBW, "wq")
            dve.wait_ge(S["ga_rs"], 2)
            dve.wait_ge(S["ga_c"], 1)
            for c in range(CH):
                v.scalar_tensor_tensor(lga[:, c, :], lga[:, c, :], vec[:, V_GKG + c:V_GKG + c + 1], rsg,
                                       ALU.mult, ALU.mult).then_inc(S["ga_n"], 1)
            dve.wait_ge(S["ga_n"], 2)
            for c in range(CH):
                v.tensor_scalar(lga[:, c, :], lga[:, c, :], vec[:, V_GKB + c:V_GKB + c + 1], None,
                                ALU.add).then_inc(S["ga_n"], 1)
            gs = ps[:, 2, :].rearrange("p (j w t) -> p j w t", j=CH, w=4)
            gvp = ps[:, 3, :].rearrange("p (j w t) -> p j w t", j=CH, w=4)
            dve.wait_ge(S["ga_s"], 1)
            v.tensor_reduce(gmx[:, :, :], gs.rearrange("p j w t -> p j t w"), AX.X, ALU.max).then_inc(S["ga_max"], 1)
            dve.wait_ge(S["ga_max"], 1)
            v.tensor_tensor(ge[:, :, :, :], gs, gmx[:, :, :].unsqueeze(2).broadcast_to([P, CH, 4, IMGS]),
                            ALU.subtract).then_inc(S["ga_max"], 1)
            dve.wait_ge(S["mod_mm"], 1)
            for j in range(CH):
                v.tensor_scalar(hT0[:, j, 0:NW], ps[:, 6, j * NW:(j + 1) * NW], vec[:, V_MB + j:V_MB + j + 1], None,
                                ALU.add).then_inc(S["h0"], 1)
            dve.wait_ge(S["ga_e"], 1)
            v.tensor_reduce(gsum[:, :, :], ge[:, :, :, :].rearrange("p j w t -> p j t w"), AX.X, ALU.add
                            ).then_inc(S["ga_sum"], 1)
            dve.wait_ge(S["ga_gv"], 1)
            dve.wait_ge(S["ga_sum"], 1)
            v.tensor_tensor(ge[:, :, :, :], ge[:, :, :, :], gvp, ALU.mult).then_inc(S["ga_agg"], 1)
            dve.wait_ge(S["ga_sum"], 1)
            v.reciprocal(gsum[:, :, :], gsum[:, :, :]).then_inc(S["ga_sum"], 1)
            dve.wait_ge(S["ga_agg"], 1)
            v.tensor_reduce(gag[:, :, :], ge[:, :, :, :].rearrange("p j w t -> p j t w"), AX.X, ALU.add
                            ).then_inc(S["ga_agg"], 1)
            dve.wait_ge(S["ga_sum"], 2)
            dve.wait_ge(S["ga_agg"], 2)
            v.tensor_tensor(gag[:, :, :], gag[:, :, :], gsum[:, :, :], ALU.mult).then_inc(S["ga_agg"], 1)
            dve.wait_ge(S["ga_proj"], 1)
            for j in range(CH):
                v.tensor_scalar(hT0[:, j, NW:NT], ps[:, 7, j * IMGS:(j + 1) * IMGS], vec[:, V_CLS + j:V_CLS + j + 1],
                                vec[:, V_GPB + j:V_GPB + j + 1], ALU.add, ALU.add).then_inc(S["h0"], 1)
            dve.wait_ge(S["x_mean"], 1)
            dve.wait_ge(S["h0"], 4)
            v.tensor_tensor(xT[:, :, :], hT0[:, :, :], ps[:, 0, 0:NT].unsqueeze(1).broadcast_to([P, CH, NT]),
                            ALU.subtract).then_inc(S["x_c"], 1)
            dve.wait_ge(S["x_rs"], 2)
            dve.wait_ge(S["x_c"], 1)
            for c in range(CH):
                v.tensor_tensor(xT[:, c, :], xT[:, c, :], rs[:, :], ALU.mult).then_inc(S["x"], 1)

            def normed(l, half, at):
                dve.wait_ge(S["n_rs"], EACH["n_rs"] * l + 2 * half + 2)
                dve.wait_ge(S["x"], EACH["x"] * l + 2 + 2 * half)
                for c in range(CH):
                    w = vec[:, at + 2 * l + c:at + 2 * l + c + 1]
                    v.scalar_tensor_tensor(hT[:, c, :], xT[:, c, :], w, rs[:, :], ALU.mult, ALU.mult
                                           ).then_inc(S["h"], 1)

            def layer(l):
                normed(l, 0, V_N1)
                dve.wait_ge(S["silu"], EACH["silu"] * l + 10)
                v.scalar_tensor_tensor(bv[:, :, :], tb.unsqueeze(2).broadcast_to([P, NG, DH]), 1.0, vs[:, :, :],
                                       ALU.add, ALU.mult).then_inc(S["kq"], 1)
                dve.wait_ge(S["rkq"], EACH["rkq"] * l + 2)
                v.tensor_tensor(kh[:, :, :], skq[:, 0], rkq[:, 0], ALU.mult).then_inc(S["kq"], 1)
                dve.wait_ge(S["kq"], EACH["kq"] * l + 2)
                v.scalar_tensor_tensor(kbq[:, 0], bt[:, :, :], 1.0, kh[:, :, :], ALU.add, ALU.mult
                                       ).then_inc(S["kq"], 1)
                dve.wait_ge(S["rkq"], EACH["rkq"] * l + 4)
                v.tensor_tensor(kbq[:, 1], skq[:, 1], rkq[:, 1], ALU.mult).then_inc(S["kq"], 1)
                v.tensor_copy(tc_[:, :, :], ic.unsqueeze(1).broadcast_to([P, NG, 32])).then_inc(S["kq"], 1)
                for i, (pj, n) in enumerate(((0, 2), (2, 2), (4, 1))):
                    b = 4 * (i % 2)
                    dve.wait_ge(S["ap_mm"], EACH["ap_mm"] * l + i + 1)
                    v.tensor_tensor(apm[:, 4 * pj:4 * (pj + n), :].rearrange("p (j h) n -> p h j n", h=HP),
                                    ps[:, b:b + 4, 0:n * P].rearrange("p h (j n) -> p h j n", j=n),
                                    map_.unsqueeze(1).unsqueeze(1).broadcast_to([P, HP, n, P]), ALU.mult
                                    ).then_inc(S["ap"], 1)
                dve.wait_ge(S["kq"], EACH["kq"] * l + 5)
                for lev in range(LEVELS):
                    m = cst[:, K_LV + 32 * lev:K_LV + 32 * lev + 32].bitcast(I32)
                    for b in range(2):
                        g = slice(NB * b, NB * (b + 1))
                        i = 2 * (2 * lev + b)
                        if lev == 0:
                            dve.wait_ge(S["y_mm"], EACH["y_mm"] * l + b + 1)
                        else:
                            dve.wait_ge(S["z_mm"], EACH["z_mm"] * l + 2 * (lev - 1) + b + 1)
                            dve.wait_ge(S["t"], EACH["t"] * l + i - 2)
                        v.copy_predicated(tc_[:, g, :], m.unsqueeze(1).broadcast_to([P, NB, 32]),
                                          bank32(b if lev == 0 else 2 + b, slice(0, P))).then_inc(S["t"], 1)
                        dve.wait_ge(S["t"], EACH["t"] * l + i + 1)
                        v.transpose(ttc[:, g, :].rearrange("p g n -> p (g n)"),
                                    tc_[:, g, :].rearrange("p g n -> p (g n)")).then_inc(S["t"], 1)
                dve.wait_ge(S["u1_mm"], EACH["u1_mm"] * l + 2)
                v.tensor_copy(both(uc, 2), ps[64:96, 4:6, 0:NT]).then_inc(S["u1_two"], 1)
                for a in range(2):
                    dve.wait_ge(S["r_mm"], EACH["r_mm"] * l + a + 1)
                    q = 2 * a + 1
                    v.tensor_tensor(both(bv, q), both(bv, q), ps[32 * q:32 * q + 32, 6:8, 0:NT], ALU.add
                                    ).then_inc(S["b2"], 1)
                dve.wait_ge(S["u2_mm"], EACH["u2_mm"] * l + 2)
                v.tensor_copy(both(uc, 3), ps[96:128, 4:6, 0:NT]).then_inc(S["u2_two"], 1)
                dve.wait_ge(S["osq"], EACH["osq"] * l + 1)
                v.tensor_reduce(oss[:, :], osq[:, :, :], AX.X, ALU.add).then_inc(S["oss"], 1)
                dve.wait_ge(S["ors"], EACH["ors"] * l + 2)
                v.tensor_tensor(osb[:, :, :].rearrange("p (a g) n -> p a g n", a=2),
                                ps[:, 6:8, 0:NT].rearrange("p a (g n) -> p a g n", n=32),
                                oss[:, :].rearrange("p (a g) -> p a g", a=2).unsqueeze(3).broadcast_to([P, 2, NB, DH]),
                                ALU.mult).then_inc(S["on"], 1)
                dve.wait_ge(S["o_t"], EACH["o_t"] * l + 1)
                onw = vec[:, V_ON + l:V_ON + l + 1]
                for p in range(3):
                    src = (ps[:, 2 * 0 + 1, :].rearrange("p (s j n) -> p s j n", s=2, j=2)[:, p] if p < 2 else
                           ps[:, 2, 0:P].rearrange("p (j n) -> p j n", j=2))
                    v.tensor_scalar(oT[:, :, P * p:min(P * p + P, NT)], src, onw, None, ALU.mult
                                    ).then_inc(S["oT"], 1)
                for j in range(CH):
                    dve.wait_ge(S["wo_mm"], EACH["wo_mm"] * l + j + 1)
                    v.tensor_tensor(xT[:, j, :], xT[:, j, :], ps[:, 3 + j, 0:NT], ALU.add).then_inc(S["x"], 1)
                normed(l, 1, V_N2)
                for i in range(FC):
                    dve.wait_ge(S["sg"], EACH["sg"] * l + i + 1)
                    r = slice(0, P) if i < FC - 1 else slice(64, P)
                    b = 3 + i % 3 if i < FC - 1 else i % 3
                    v.tensor_tensor(act[r, i, :], sg[r, i % 2, :], ps[r, b, 0:NT], ALU.mult).then_inc(S["act"], 1)
                for j in range(CH):
                    dve.wait_ge(S["dn_mm"], EACH["dn_mm"] * l + j + 1)
                    v.tensor_tensor(xT[:, j, :], xT[:, j, :], ps[:, 6 + j, 0:NT], ALU.add).then_inc(S["x"], 1)

            for l in range(LAYERS):
                layer(l)

            dve.wait_ge(S["fin_rs"], 2)
            dve.wait_ge(S["x"], EACH["x"] * LAYERS + 2)
            for c in range(CH):
                v.scalar_tensor_tensor(xT[:, c, :], xT[:, c, :], vec[:, V_FW + c:V_FW + c + 1], rs[:, :], ALU.mult,
                                       ALU.mult).then_inc(S["fin_y"], 1)
            dve.wait_ge(S["fin_y"], 2)
            v.tensor_tensor(hT0[:, :, :], hT0[:, :, :], xT[:, :, :], ALU.add).then_inc(S["fin_y"], 1)
            dve.wait_ge(S["h1"], 2)
            for p in range(3):
                v.bn_stats(stt[:, p, :], h1[:, p, :]).then_inc(S["stats"], 1)
            for p in range(3):
                dve.wait_ge(S["stats"], p + 1)
                v.bn_aggr(mv[:, p, :], stt[:, p, :]).then_inc(S["stats"], 1)
            dve.wait_ge(S["rs3"], 2)
            dve.wait_ge(S["stats"], 6)
            for p in range(3):
                v.tensor_scalar(xn[:, p, :], h1[:, p, :], mv[:, p, 0:1], rs3[:, p:p + 1], ALU.subtract, ALU.mult
                                ).then_inc(S["xn"], 1)
            dve.wait_ge(S["xn"], 3)
            quantize(xn[:, :, :].rearrange("p t n -> p (t n)"), 48, "xq")
            for p in range(3):
                n = P if p < 2 else 64
                dve.wait_ge(S["gate"], p + 1)
                b = 4 * (p % 2)
                v.tensor_tensor(hh[0:n, p, :].rearrange("p (a n) -> p a n", a=2),
                                sgu[0:n, :].rearrange("p (a n) -> p a n", a=2), ps[0:n, b + 2:b + 4, 0:352],
                                ALU.mult).then_inc(S["hh"], 1)
                dve.wait_ge(S["hh"], p + 1)
                quantize(hh[0:n, p, :], NBW, "hq")
            for p in range(3):
                n = P if p < 2 else 64
                dve.wait_ge(S["out_mm"], p + 1)
                v.tensor_tensor(h1[0:n, p, :], h1[0:n, p, :], ps[0:n, 6 + p % 2, 0:C], ALU.add
                                ).then_inc(S["outs"], 1)

        @blk_.tensor
        def _(pe):
            mm = nc.tensor.matmul

            def norm_sum(out_, src, weights):
                for c in range(CH):
                    last = mm(out_, weights, src[:, c], start=(c == 0), stop=(c == CH - 1))
                return last

            def conv(g):
                pe.wait_ge(s_x[g], 16)
                for c in range(CH):
                    i = 2 * g + c
                    if i >= 4:
                        pe.wait_ge(S["copied"], i - 3)
                    for k in range(KC):
                        last = mm(ps[:, i % 4, 0:GRP], cwc[:, k, c * P:(c + 1) * P], xg[:, g, k, :],
                                  start=(k == 0), stop=(k == KC - 1))
                    last.then_inc(S["conv"], 1)

            def red(hf):
                pe.wait_ge(S["xsum"], 8 * hf + 8)
                if hf:
                    pe.wait_ge(S["red"], hf)
                for c in range(CH):
                    for k in range(KC):
                        last = mm(ps[:, 4, c * P:(c + 1) * P], cw[:, k, c * P:(c + 1) * P], xs[:, hf, k, :],
                                  start=(k == 0), stop=(k == KC - 1))
                last.then_inc(S["red_mm"], 1)

            def red_mean(hf):
                pe.wait_ge(S["red"], hf + 1)
                if hf:
                    pe.wait_ge(S["q"], hf)
                norm_sum(ps[:, 5, 0:P], redT[:, :, hf * P:(hf + 1) * P], ones[:, :]).then_inc(S["mean_mm"], 1)

            def red_var(hf):
                pe.wait_ge(S["csq"], hf + 1)
                norm_sum(ps[:, 5, P:2 * P], redq[:, :, :], ones[:, :]).then_inc(S["var_mm"], 1)

            def query(hf):
                pe.wait_ge(S["lnq"], 4 * hf + 4)
                for c in range(CH):
                    last = mm(ps[:, 5, C:2 * C], lnq[:, c, :], tw(T_Q)[:, c, :], start=(c == 0), stop=(c == CH - 1))
                last.then_inc(S["q_mm"], 1)

            def stat(hf):
                pe.wait_ge(S["squared"], 6 * hf + 6)
                for t in range(NP_):
                    for c in range(CH):
                        last = mm(ps[:, 7 - hf, t:t + 1], sq[:, c, t * P:(t + 1) * P], ones[:, 0:1],
                                  start=(c == 0), stop=(c == CH - 1))
                last.then_inc(S["stat_mm"], 1)

            def kv(un):
                hf, uu = divmod(un, 5)
                n = min(2, NP_ - 2 * uu)
                if un >= 2:
                    pe.wait_ge(S["k_used"], K_AT[un - 2])
                    pe.wait_ge(S["v_kept"], un - 1)
                for w in range(2):
                    for t in range(n):
                        i = NP_ * hf + 2 * uu + t
                        for c in range(CH):
                            last = mm(ps[:, 2 * w + un % 2, t * C:(t + 1) * C], pecT[:, c, i * P:(i + 1) * P],
                                      wkvg[:, c, w * C:(w + 1) * C], start=(c == 0), stop=(c == CH - 1))
                last.then_inc(S["kv_mm"], 1)

            K_AT = [2 + 2 * (un + 1) + (4 if un >= 5 else 0) for un in range(10)]

            pe.wait_ge(S["cwc"], 3)
            conv(0)
            pe.wait_ge(S["ones"], 1)
            pe.wait_ge(S["vecs"], 16)
            norm_sum(ps[:, 7, 0:1], vec[:, V_CLS:V_CLS + 2].unsqueeze(2), ones[:, :]).then_inc(S["cls_mm"], 1)
            conv(1)
            pe.wait_ge(S["cls_v"], 1)
            norm_sum(ps[:, 7, 8:9], clsv[:, 2:4].unsqueeze(2), ones[:, :]).then_inc(S["cls_mm"], 1)
            pe.wait_ge(S["tokw"], 16)
            for c in range(CH):
                last = mm(ps[:, 6, :], vec[:, V_LKB + c:V_LKB + c + 1].broadcast_to([P, P]), wkv[:, c, :],
                          start=(c == 0), stop=(c == CH - 1))
            last.then_inc(S["kvb_mm"], 1)
            conv(2)
            pe.wait_ge(S["cls_n"], 3)
            pe.wait_ge(S["kvb"], 1)
            for c in range(CH):
                last = mm(ps[:, 6, 0:C], clsv[:, 6 + c:7 + c].broadcast_to([P, P]), tw(T_GQ)[:, c, :],
                          start=(c == 0), stop=(c == CH - 1))
            last.then_inc(S["gq_mm"], 1)
            conv(3)
            pe.wait_ge(S["cls_v"], 3)
            pe.wait_ge(S["cls_c"], 1)
            stat(0)
            red(0)
            red_mean(0)
            conv(4)
            red_var(0)
            conv(5)
            query(0)
            red(1)
            pe.wait_ge(S["wkvg"], 2)
            pe.wait_ge(S["copied"], 12)
            kv(0)
            red_mean(1)
            kv(1)
            red_var(1)
            kv(2)
            query(1)
            pe.wait_ge(S["u"], 2)
            stat(1)
            for un in range(3, 8):
                kv(un)

            def to_channels(hf):
                pe.wait_ge(S["agg"], 2 * hf + 2)
                if hf:
                    pe.wait_ge(S["aggT"], hf)
                else:
                    pe.wait_ge(S["red"], 2)
                for c in range(CH):
                    last = nc.tensor.transpose(ps[:, 4, c * P:(c + 1) * P], agg[:, c * P:(c + 1) * P], ident)
                last.then_inc(S["aggr_t"], 1)

            def project(hf):
                pe.wait_ge(S["aggT"], hf + 1)
                if hf:
                    pe.wait_ge(S["loc"], 2 * hf)
                else:
                    pe.wait_ge(S["q"], 2)
                for j in range(CH):
                    for c in range(CH):
                        last = mm(ps[:, 5, j * P:(j + 1) * P], tw(T_PR)[:, c, j * P:(j + 1) * P], aggT[:, c, :],
                                  start=(c == 0), stop=(c == CH - 1))
                last.then_inc(S["proj_mm"], 1)

            to_channels(0)
            kv(8)
            project(0)
            kv(9)
            to_channels(1)
            project(1)
            pe.wait_ge(S["loc"], 4)
            pe.wait_ge(S["k_used"], K_AT[8])
            norm_sum(ps[:, 0, 0:NW], locT[:, :, :], ones[:, :]).then_inc(S["ga_mean"], 1)
            pe.wait_ge(S["k_used"], K_AT[9])
            pe.wait_ge(S["v_kept"], 10)
            pe.wait_ge(S["ga_sq"], 1)
            norm_sum(ps[:, 1, 0:NW], lga2[:, :, :], ones[:, :]).then_inc(S["ga_var"], 1)
            pe.wait_ge(S["rk"], 4)
            for j in range(CH):
                for c in range(CH):
                    last = mm(ps[:, 6, j * NW:(j + 1) * NW], tw(T_MOD)[:, c, j * P:(j + 1) * P], locT[:, c, :],
                              start=(c == 0), stop=(c == CH - 1))
            last.then_inc(S["mod_mm"], 1)
            pe.wait_ge(S["ga_n"], 4)
            pe.wait_ge(S["u"], 4)
            for j in range(CH):
                for c in range(CH):
                    last = mm(ps[:, 2, j * NW:(j + 1) * NW],
                              ux[:, c, HP * j:HP * (j + 1), :].rearrange("p h d -> p (h d)"), lga[:, c, :],
                              start=(c == 0), stop=(c == CH - 1))
            last.then_inc(S["ga_s"], 1)
            for j in range(CH):
                for c in range(CH):
                    last = mm(ps[:, 3, j * NW:(j + 1) * NW], gwkv[:, c, C + j * P:C + (j + 1) * P], lga[:, c, :],
                              start=(c == 0), stop=(c == CH - 1))
            last.then_inc(S["ga_gv"], 1)
            pe.wait_ge(S["wq"], 6)
            pe.wait_ge(S["aggT"], 2)
            pe.wait_ge(S["loc"], 4)
            for i in range(9):
                b = 4 + i % 2
                if i >= 2:
                    pe.wait_ge(S["wqT"], i - 1)
                if i < 6:
                    for k in range(min(4, 22 - 4 * i)):
                        r, c = 2 * i + k // 2, k % 2
                        last = nc.tensor.transpose(ps[:, b, k * P:(k + 1) * P], wf[:, r * C + c * P:r * C + c * P + P],
                                                   ident)
                else:
                    for k in range(4):
                        kk, nn = 2 * (i - 6) + k // 2, k % 2
                        at = 4 * INTER + nn * INTER + kk * P
                        w = min(P, INTER - kk * P)
                        last = nc.tensor.transpose(ps[0:w, b, k * P:(k + 1) * P], wf[:, at:at + w], ident)
                last.then_inc(S["wq_t"], 1)
            pe.wait_ge(S["ga_agg"], 3)
            for j in range(CH):
                for c in range(CH):
                    last = mm(ps[:, 7, j * IMGS:(j + 1) * IMGS], tw(T_GP)[:, c, j * P:(j + 1) * P], gag[:, c, :],
                              start=(c == 0), stop=(c == CH - 1))
            last.then_inc(S["ga_proj"], 1)
            pe.wait_ge(S["h0"], 4)
            norm_sum(ps[:, 0, 0:NT], hT0[:, :, :], ones[:, :]).then_inc(S["x_mean"], 1)
            pe.wait_ge(S["x_sq"], 1)
            norm_sum(ps[:, 1, 0:NT], sqx[:, :, :], ones[:, :]).then_inc(S["x_var"], 1)
            pe.wait_ge(S["wqT"], 10)
            pe.wait_ge(S["x_rs"], 1)

            def norm(l, half):
                pe.wait_ge(S["n_sq"], EACH["n_sq"] * l + half + 1)
                norm_sum(ps[:, 0, 0:NT], sqx[:, :, :], ones[:, :]).then_inc(S["n_ms"], 1)

            def project_to(bank, w, j):
                for c in range(CH):
                    last = mm(ps[:, bank, 0:NT], w(c, j), hT[:, c, :], start=(c == 0), stop=(c == CH - 1))
                return last

            def layer(l):
                pe.wait_ge(S["lwa"], 16 * l + 16)
                pe.wait_ge(S["consts"], 16)
                norm(l, 0)
                pe.wait_ge(S["h"], EACH["h"] * l + 2)
                for at, b, name in ((L_K, 1, "k_mm"), (L_Q, 3, "q2_mm")):
                    for j in range(CH):
                        last = project_to(b + j, lambda c, j: lw(at)[:, c, j * P:(j + 1) * P], j)
                    last.then_inc(S[name], 1)
                pe.wait_ge(S["wbx"], EACH["wbx"] * l + 1)
                for j in range(CH):
                    last = project_to(5 + j, lambda c, j: wbx[:, c, HP * j:HP * (j + 1), :].rearrange(
                        "p h d -> p (h d)"), j)
                last.then_inc(S["bt_mm"], 1)
                pe.wait_ge(S["n_rs"], EACH["n_rs"] * l + 2)
                for bank, at, p in ((7, 0, 0), (0, 0, 1)):
                    for c in range(CH):
                        last = mm(ps[:, bank, at:at + 264], hT[:, c, P * p:P * p + P],
                                  wvb[:, c].rearrange("p j n -> p (j n)"), start=(c == 0), stop=(c == CH - 1))
                for a in range(2):
                    for c in range(CH):
                        last = mm(ps[64 * a:64 * a + 64, 7, 264:396], hT[:, c, NW:NT], wvb[:, c, a, :],
                                  start=(c == 0), stop=(c == CH - 1))
                last.then_inc(S["v_mm"], 1)
                for a in range(2):
                    pe.wait_ge(S["silu"], EACH["silu"] * l + a + 3)
                    for j in range(CH):
                        last = mm(ps[:, 1 + 2 * a + j, 0:NT], blk, kqsq[:, a, j, :], start=True, stop=True)
                    last.then_inc(S["ss_mm"], 1)
                pe.wait_ge(S["kq"], EACH["kq"] * l + 4)
                pe.wait_ge(S["silu"], EACH["silu"] * l + 10)
                for pj in range(PJ):
                    if pj == 4:
                        pe.wait_ge(S["ap"], EACH["ap"] * l + 1)
                    for a in range(2):
                        sq_, j = (2 * (pj // 2) + a, pj % 2) if pj < 4 else (4, a)
                        for h in range(HP):
                            r = slice(DH * h, DH * h + DH)
                            at = slice(IMGS * sq_, IMGS * sq_ + IMGS)
                            last = mm(ps[64 * a:64 * a + 64, 4 * (pj // 2 % 2) + h, P * (pj % 2):P * (pj % 2) + P],
                                      kh[r, j, at], kbq[r, :, j, at], start=True, stop=True)
                    if pj != 0 and pj != 2:
                        last.then_inc(S["ap_mm"], 1)
                pe.wait_ge(S["ap"], EACH["ap"] * l + 3)
                pe.wait_ge(S["kq"], EACH["kq"] * l + 5)
                for lev in range(LEVELS):
                    for b in range(2):
                        if lev:
                            pe.wait_ge(S["t"], EACH["t"] * l + 2 * (2 * (lev - 1) + b + 1))
                        for k in range(NB):
                            for q in range(4):
                                r = slice(32 * q, 32 * q + 32)
                                own = slice(32 * (q % 2), 32 * (q % 2) + 32)
                                last = mm(ps[r, b, 32 * k:32 * k + 32], apm[r, NB * b + k, own],
                                          tc_[r, NB * b + k, :] if lev else ic[r, :], start=True, stop=True)
                        last.then_inc(S["y_mm"], 1)
                    for b in range(2):
                        if lev:
                            pe.wait_ge(S["y"], EACH["y"] * l + 2 * (lev - 1) + b + 1)
                            for k in range(NB):
                                for q in range(4):
                                    r = slice(32 * q, 32 * q + 32)
                                    last = mm(ps[r, 2 + b, 32 * k:32 * k + 32], ttc[r, NB * b + k, :],
                                              yc[r, NB * b + k, :], start=True, stop=True)
                            last.then_inc(S["z_mm"], 1)

                def solve(q, rhs):
                    r = slice(32 * q, 32 * q + 32)
                    for g in range(NG):
                        last = mm(ps[r, 4 + g // NB, 32 * (g % NB):32 * (g % NB) + 32], ttc[r, g, :], rhs[r, g, :],
                                  start=True, stop=True)
                    return last

                pe.wait_ge(S["t"], EACH["t"] * l + 4 * LEVELS)
                for a in range(2):
                    solve(2 * a, bv).then_inc(S["u1_mm"], 1)
                for a in range(2):
                    pe.wait_ge(S["u1_two" if a else "u1"], l + 1)
                    for g in range(NG):
                        last = mm(ps[64 * a + 32:64 * a + 64, 6 + g // NB, 32 * (g % NB):32 * (g % NB) + 32],
                                  apm[64 * a:64 * a + 32, g, 32:64], uc[64 * a:64 * a + 32, g, :],
                                  start=True, stop=True)
                    last.then_inc(S["r_mm"], 1)
                for a in range(2):
                    pe.wait_ge(S["b2"], EACH["b2"] * l + a + 1)
                    solve(2 * a + 1, bv).then_inc(S["u2_mm"], 1)
                pe.wait_ge(S["b2"], EACH["b2"] * l + 2)
                for a in range(2):
                    pe.wait_ge(S["u2_two" if a else "u2"], l + 1)
                    r = slice(64 * a, 64 * a + 64)
                    for g in range(NG):
                        last = mm(ps[r, 6 + g // NB, 32 * (g % NB):32 * (g % NB) + 32], apm[r, g, 64:P], uc[r, g, :],
                                  start=True, stop=True)
                last.then_inc(S["o_mm"], 1)
                pe.wait_ge(S["on"], EACH["on"] * l + 1)
                for pj in range(PJ):
                    o_ = ps[:, 1, P * pj:P * pj + P] if pj < 4 else ps[:, 2, 0:P]
                    last = nc.tensor.transpose(o_, osb[:, 4 * pj:4 * pj + 4, :].rearrange("p g n -> p (g n)"), ident)
                last.then_inc(S["o_t"], 1)
                pe.wait_ge(S["oT"], EACH["oT"] * l + 3)
                for j in range(CH):
                    for c in range(CH):
                        last = mm(ps[:, 3 + j, 0:NT], lw(L_O)[:, c, j * P:(j + 1) * P], oT[:, c, :],
                                  start=(c == 0), stop=(c == CH - 1))
                    last.then_inc(S["wo_mm"], 1)
                norm(l, 1)
                pe.wait_ge(S["lwb"], 16 * l + 16)
                pe.wait_ge(S["h"], EACH["h"] * l + 4)
                pe.wait_ge(S["n_rs"], EACH["n_rs"] * l + 3)
                for i in range(FC):
                    if i >= 3:
                        pe.wait_ge(S["act"], EACH["act"] * l + i - 2)
                    if i < FC - 1:
                        project_to(i % 3, lambda c, j: wg[:, c, i * P:(i + 1) * P], 0)
                        last = project_to(3 + i % 3, lambda c, j: wg[:, c, 640 + i * P:640 + (i + 1) * P], 0)
                    else:
                        last = project_to(i % 3, lambda c, j: wg[:, c, 1280:1408], 0)
                    last.then_inc(S["up_mm"], 1)
                pe.wait_ge(S["on"], EACH["on"] * l + 1)
                pe.wait_ge(S["zeros"], 2)
                for j in range(CH):
                    for i in range(FC):
                        if j == 0:
                            pe.wait_ge(S["act"], EACH["act"] * l + i + 1)
                        last = mm(ps[:, 6 + j, 0:NT], wd[:, i, j * P:(j + 1) * P], act[:, i, :],
                                  start=(i == 0), stop=(i == FC - 1))
                    last.then_inc(S["dn_mm"], 1)

            for l in range(LAYERS):
                layer(l)

            pe.wait_ge(S["fin_sq"], 1)
            norm_sum(ps[:, 0, 0:NT], sqx[:, :, :], ones[:, :]).then_inc(S["fin_ms"], 1)
            pe.wait_ge(S["fin_y"], 3)
            for p in range(3):
                n = P if p < 2 else 64
                for c in range(CH):
                    o_ = ps[:, 1, C * p + c * P:C * p + (c + 1) * P] if p < 2 else ps[0:64, 2, c * P:(c + 1) * P]
                    last = nc.tensor.transpose(o_, hT0[:, c, P * p:P * p + n], ident)
            last.then_inc(S["h1_t"], 1)
            pe.wait_ge(S["xq"], 1)
            for p in range(3):
                n = P if p < 2 else 64
                for c in range(CH):
                    o_ = ps[:, 3, C * p + c * P:C * p + (c + 1) * P] if p < 2 else ps[:, 4, 64 * c:64 * c + 64]
                    last = nc.tensor.transpose(o_, xn[0:n, p, c * P:(c + 1) * P], ident[0:n, 0:n])
            last.then_inc(S["xq_t"], 1)
            pe.wait_ge(S["xqT"], 2)
            pe.wait_ge(S["h1"], 2)
            for p in range(3):
                n = P if p < 2 else 64
                if p == 2:
                    pe.wait_ge(S["hh"], 1)
                b = 4 * (p % 2)
                for w in range(4):
                    for c in range(CH):
                        last = mm(ps[0:n, b + w, 0:352], xqT[:, c, P * p:P * p + n],
                                  wguT[:, c, 352 * w:352 * w + 352], start=(c == 0), stop=(c == CH - 1))
                last.then_inc(S["gu_mm"], 1)
            pe.wait_ge(S["hh"], 3)
            for p in range(3):
                n = P if p < 2 else 64
                pe.wait_ge(S["hq"], p + 1)
                for k in range(FC):
                    w = min(P, INTER - k * P)
                    at = k * n
                    o_ = ps[0:w, 2 * p, at:at + n] if k < 4 else ps[0:w, 2 * p + 1, at - 4 * n:at - 3 * n]
                    last = nc.tensor.transpose(o_, hh[0:n, p, k * P:k * P + w], ident[0:n, 0:n])
                last.then_inc(S["hq_t"], 1)
                pe.wait_ge(S["hqT"], 3 * p + 3)
                if p == 2:
                    pe.wait_ge(S["outs"], 1)
                for k in range(FC):
                    w = min(P, INTER - k * P)
                    last = mm(ps[0:n, 6 + p % 2, 0:C], hqT[0:w, k, P * p:P * p + n], wdT[0:w, k, :],
                              start=(k == 0), stop=(k == FC - 1))
                last.then_inc(S["out_mm"], 1)


def constants():
    import numpy as np
    i = np.arange(P)
    s, t = i[:, None], i[None, :]
    c = np.zeros((P, NK), np.float32)
    c[:, K_ID:K_ID + P] = s == t
    c[:, K_BLK:K_BLK + P] = s // 32 == t // 32
    c[:, K_AP:K_AP + 64] = -1.0 * (s % 64 < t[:, 0:64])
    c[:, K_AP + 64:K_AP + P] = s % 64 <= t[:, 0:64]
    r, j = (i % 32)[:, None], np.arange(32)[None, :]
    c[:, K_IC:K_IC + 32] = r == j
    for lev in range(LEVELS):
        b = 1 << lev
        c[:, K_LV + 32 * lev:K_LV + 32 * lev + 32] = (r // (2 * b) == j // (2 * b)) & (r // b % 2 == 1) & (j // b % 2 == 0)
    return c


def kernel(**inputs):
    import numpy as np
    import concourse.bacc as bacc
    from concourse.bass_utils import run_bass_kernel_spmd

    def a(name):
        return np.asarray(inputs[name])

    def rows(w, chunks):
        return w.reshape(chunks, P, -1).transpose(1, 0, 2).reshape(P, -1)

    x = a("x").reshape(IMGS, 3, 2, 3, 14, 2, 3, 14).transpose(1, 4, 7, 2, 3, 6, 5, 0).reshape(588, 6, GRP)
    xp = np.zeros((KC * KP, 6, GRP), np.float32)
    xp[:588] = x
    xp = xp.reshape(KC, KP, 6, GRP).transpose(2, 1, 0, 3)
    cw = np.zeros((KC * KP, C), np.float32)
    cw[:588] = a("L0_tok_conv_w").reshape(C, 588).T
    cw = cw.reshape(KC, KP, C).transpose(1, 0, 2)

    def vector(w):
        return w.reshape(CH, P).T

    t = "L0_tok_"
    cols = [vector(a(t + n)) for n in ("class_emb", "la_ln_q_g", "la_ln_q_b", "la_ln_kv_g", "la_ln_kv_b", "la_proj_b",
                                       "ga_ln_q_g", "ga_ln_q_b", "ga_ln_kv_g", "ga_ln_kv_b", "ga_proj_b", "mod_b")]
    for n in ("norm1_w", "norm2_w"):
        cols += [vector(a("L0_attn_" + n)[l]) for l in range(LAYERS)]
    cols.append(vector(a("L0_attn_final_norm_w")))
    cols += [np.tile(a("L0_attn_onorm_w")[l], HP)[:, None] for l in range(LAYERS)]
    vec = np.concatenate(cols, 1)
    wt = np.concatenate([rows(a(t + n), CH) for n in ("la_wkv", "la_wq", "la_proj_w", "ga_wq", "ga_wkv", "ga_proj_w",
                                                      "mod_w")], 1)
    layers = []
    for l in range(LAYERS):
        wq, wk, wv, wb, wo, wg, wd = (a("L0_attn_" + n)[l] for n in ("Wq", "Wk", "Wv", "Wb", "Wo", "Wg", "Wd"))
        wvb = np.concatenate([wv[:, 0:P], wb[:, 0:4], wv[:, P:C], wb[:, 4:8]], 1)
        wg = np.concatenate([wg[:, 0:640], wg[:, 704:1344], wg[:, 640:704], wg[:, 1344:1408]], 1)
        wdp = np.concatenate([wd[0:640], np.zeros((64, C), np.float32), wd[640:704]], 0)
        layers.append(np.concatenate([rows(w, len(w) // P) for w in (wq, wk, wvb, wb, wo, wg, wdp)], 1))
    wl = np.stack(layers)
    f = "L0_ffn_"
    wf = np.concatenate([rows(np.concatenate([a(f + "w_gate"), a(f + "w_up")], 0), 11), rows(a(f + "w_down"), CH)], 1)

    arrays = {"in_patches": xp, "in_conv": cw, "in_vectors": vec, "in_tok": wt, "in_layers": wl, "in_ffn": wf,
              "in_constants": constants()}
    nc = bacc.Bacc("TRN2", target_bir_lowering=False, num_devices=1)
    args = []
    for name, arr in arrays.items():
        arrays[name] = np.ascontiguousarray(arr)
        args.append(nc.dram_tensor(name, arr.shape, F32, kind="ExternalInput").ap())
    out = nc.dram_tensor("out", (IMGS, SLOTS, C), F32, kind="ExternalOutput").ap()
    build(nc, *args, out)
    r = run_bass_kernel_spmd(nc, [arrays], core_ids=[0])
    return r.results[0]["out"]
```
